# Optimizing a Trainium2 kernel written in Bass

```python
import numpy as np
import jax
import jax.numpy as jnp

def _softmax(x, axis=-1):
    return jax.nn.softmax(x, axis=axis)

def _gelu(x):
    return jax.nn.gelu(x, approximate=True)

def _silu(x):
    return jax.nn.silu(x)

def _sigmoid(x):
    return jax.nn.sigmoid(x)

def _layernorm(x, axis=-1, eps=1e-05):
    m = jnp.mean(x, axis=axis, keepdims=True)
    v = jnp.var(x, axis=axis, keepdims=True)
    return (x - m) / jnp.sqrt(v + eps)

def _scatter_add(tgt, idx, src, axis=0):
    return tgt.at[idx].add(src)

def _segment_sum(src, seg, n):
    return jax.ops.segment_sum(src, seg, n)
kernel_name = 'mk_gnn_preln_d1_gnn_r8_f166b4'

def setup_inputs(seed: int=0):
    np.random.seed(seed)
    _w = jnp.asarray

    def _rec_inputs():
        import jax
        import jax.numpy as jnp
        _gk = jax.random.key(seed)
        x = -0.000202 + 1 * jax.random.normal(jax.random.fold_in(_gk, 1), (12500, 64), jnp.float32)
        src = jax.random.randint(jax.random.fold_in(_gk, 2), (400000,), 0, 12500, jnp.int32)
        dst = jnp.minimum((12500 * jax.random.uniform(jax.random.fold_in(_gk, 3), (400000,)) ** 2.0).astype(jnp.int32), 99999)
        _o = jnp.argsort(dst, stable=True)
        src = src[_o]
        dst = dst[_o]
        edge_attr_16 = 0.000283511 + 1.00007 * jax.random.normal(jax.random.fold_in(_gk, 11), (400000, 16), jnp.float32)
        return (x, src, dst, edge_attr_16)
    x, src, dst, edge_attr_16 = _rec_inputs()

    def _L0_gnn_setup():
        import jax, jax.numpy as jnp
        import numpy as np
        N_NODES = 12500
        N_EDGES = 150000
        HIDDEN = 64
        EDGE_DIM = 16
        LN_EPS = 1e-06
        key = jax.random.key(seed)
        ks = jax.random.split(key, 10)
        node_features = jax.random.normal(ks[0], (N_NODES, HIDDEN), dtype=jnp.float32)
        edge_index = jax.random.randint(ks[1], (2, N_EDGES), 0, N_NODES, dtype=jnp.int64)
        edge_features = jax.random.normal(ks[2], (N_EDGES, EDGE_DIM), dtype=jnp.float32)
        s1 = 1.0 / np.sqrt(HIDDEN + EDGE_DIM)
        W1 = jax.random.normal(ks[3], (HIDDEN + EDGE_DIM, HIDDEN), dtype=jnp.float32) * s1
        b1 = jnp.zeros((HIDDEN,), dtype=jnp.float32)
        s2 = 1.0 / np.sqrt(HIDDEN)
        W2 = jax.random.normal(ks[4], (HIDDEN, HIDDEN), dtype=jnp.float32) * s2
        b2 = jnp.zeros((HIDDEN,), dtype=jnp.float32)
        s3 = 1.0 / np.sqrt(2 * HIDDEN)
        W3 = jax.random.normal(ks[5], (2 * HIDDEN, HIDDEN), dtype=jnp.float32) * s3
        b3 = jnp.zeros((HIDDEN,), dtype=jnp.float32)
        ln_scale = jnp.ones((HIDDEN,), dtype=jnp.float32)
        ln_bias = jnp.zeros((HIDDEN,), dtype=jnp.float32)
        return {'node_features': node_features, 'edge_features': edge_features, 'edge_index': edge_index, 'W1': W1, 'b1': b1, 'W2': W2, 'b2': b2, 'W3': W3, 'b3': b3, 'ln_scale': ln_scale, 'ln_bias': ln_bias}
    _L0_gnn_all = _L0_gnn_setup()
    _L0_gnn_in = {k: v for k, v in _L0_gnn_all.items() if k in ('W1', 'b1', 'W2', 'b2', 'W3', 'b3', 'ln_scale', 'ln_bias')}
    del _L0_gnn_all
    return {'x': x, 'src': src, 'dst': dst, 'edge_attr_16': edge_attr_16, 'L0_gnn_W1': _L0_gnn_in['W1'], 'L0_gnn_b1': _L0_gnn_in['b1'], 'L0_gnn_W2': _L0_gnn_in['W2'], 'L0_gnn_b2': _L0_gnn_in['b2'], 'L0_gnn_W3': _L0_gnn_in['W3'], 'L0_gnn_b3': _L0_gnn_in['b3'], 'L0_gnn_ln_scale': _L0_gnn_in['ln_scale'], 'L0_gnn_ln_bias': _L0_gnn_in['ln_bias']}

def reference(x, src, dst, edge_attr_16, L0_gnn_W1, L0_gnn_b1, L0_gnn_W2, L0_gnn_b2, L0_gnn_W3, L0_gnn_b3, L0_gnn_ln_scale, L0_gnn_ln_bias):
    import jax
    import jax.numpy as jnp

    def _L0_gnn_ref(node_features, edge_features, edge_index, W1, b1, W2, b2, W3, b3, ln_scale, ln_bias):
        import jax, jax.numpy as jnp
        import numpy as np
        N_NODES = 12500
        N_EDGES = 150000
        HIDDEN = 64
        EDGE_DIM = 16
        LN_EPS = 1e-06
        src, dst = (edge_index[0], edge_index[1])
        src_feat = node_features[src]
        msg = jnp.concatenate([src_feat, edge_features], axis=-1)
        msg = jax.nn.gelu(msg @ W1 + b1)
        msg = msg @ W2 + b2
        agg = jax.ops.segment_sum(msg, dst, num_segments=node_features.shape[0])
        upd = jnp.concatenate([node_features, agg], axis=-1)
        h = upd @ W3 + b3
        mu = jnp.mean(h, axis=-1, keepdims=True)
        var = jnp.mean(jnp.square(h - mu), axis=-1, keepdims=True)
        h = (h - mu) * jax.lax.rsqrt(var + LN_EPS) * ln_scale + ln_bias
        h = jax.nn.gelu(h)
        return h + node_features
    edge_index = jnp.stack([src, dst])
    h = jnp.maximum(_layernorm(x, axis=-1), 0.0)
    x = x + _L0_gnn_ref(h, edge_attr_16, edge_index, L0_gnn_W1, L0_gnn_b1, L0_gnn_W2, L0_gnn_b2, L0_gnn_W3, L0_gnn_b3, L0_gnn_ln_scale, L0_gnn_ln_bias)
    return x

_drawn_inputs = setup_inputs


def setup_inputs(seed=0):
    import zlib

    import numpy as np

    out = dict(_drawn_inputs(seed))
    spreads = {'L0_gnn_b1': (0.0, 0.1),
     'L0_gnn_b2': (0.0, 0.1),
     'L0_gnn_b3': (0.0, 0.773),
     'L0_gnn_ln_scale': (1.0, 0.2),
     'L0_gnn_ln_bias': (0.0, 0.1)}
    factors = {}
    for name, (base, spread) in spreads.items():
        noise = np.random.default_rng([zlib.crc32(name.encode()), seed]).standard_normal(out[name].shape)
        drawn = base * np.exp(spread * noise) if base else spread * noise
        out[name] = jnp.asarray(drawn.astype(out[name].dtype))
    for name, factor in factors.items():
        out[name] = (out[name] * factor).astype(out[name].dtype)
    return out
```

```python
from contextlib import ExitStack

import concourse.bass as bass
from concourse import mybir

F32 = mybir.dt.float32
I32 = mybir.dt.int32
ALU = mybir.AluOpType
ACT = mybir.ActivationFunctionType
AX = mybir.AxisListType

P = 128
T = 5
SLOTS = 5
W = 64
NP = 125
MAIN_P = 120
PAIRS = 5
UNIT = 4
UNITS = 5
BANK = 512
LN1_EPS = 1e-5
LN2_EPS = 1e-6


def gnn_layer(nc, x, src_t, dst_t, edge_t, w1, b1, w2_t, b2, w3, b3, ln_scale, ln_bias, out):
    N, H = x.shape
    NCH, KE, _ = edge_t.shape
    D = KE // T
    NT = NCH * T
    ROUNDS = NCH // SLOTS
    NJ = N // NP
    BJ = 2 * PAIRS
    NB = NJ // BJ
    FJ = UNIT * UNITS
    FB = NJ // FJ
    Q = max(d for d in range(1, P + 1) if NCH % d == 0)
    QS = NCH // Q
    SHIFT = W.bit_length() - 1
    assert NCH % SLOTS == 0 and NJ % (2 * BJ) == 0 and NJ % FJ == 0 and QS <= 8 and NCH <= 2 * BANK

    table = nc.dram_tensor("table", (N, H), F32, kind="Internal").ap()
    x_v = x.rearrange("(p j) h -> p (j h)", p=NP)
    table_v = table.rearrange("(p j) h -> p (j h)", p=NP)
    out_v = out.rearrange("(p j) h -> p (j h)", p=NP)
    parts = [(0, MAIN_P), (MAIN_P, NP)]

    with ExitStack() as ctx:
        def sb(name, shape, dt=F32):
            return ctx.enter_context(nc.sbuf_tensor(name, shape, dt))

        def sem(name):
            return ctx.enter_context(nc.semaphore(name))

        xr = sb("xr", [NP, NJ * H])
        hq = sb("hq", [NP, NJ * H])
        h_blk = sb("h_blk", [NP, 2, BJ * H])
        hT = sb("hT", [P, 2, PAIRS, NP])
        t_blk = sb("t_blk", [NP, 2, BJ * H])
        sq = sb("sq", [NP, 2, BJ * H])
        mean = sb("mean", [NP, NJ])
        total = sb("total", [NP, NJ])
        var = sb("var", [NP, NJ])
        std = sb("std", [NP, NJ])
        rstd = sb("rstd", [NP, NJ])
        w_edge = sb("w_edge", [KE + 1, T * H])
        w_node = sb("w_node", [P, 4 * H])
        w3a = sb("w3a", [2 * H, H])
        w3b = sb("w3b", [H, H])
        w3c = sb("w3c", [2 * H, H])
        w3bc = sb("w3bc", [H, H])
        w2b = sb("w2b", [H, H + 1])
        w_agg = sb("w_agg", [H + 1, H])
        wsum = sb("wsum", [P, 4])
        b3_row = sb("b3_row", [NP, H])
        b3_c = sb("b3_c", [NP, H])
        scale_row = sb("scale_row", [NP, H])
        bias_row = sb("bias_row", [NP, H])
        eps = sb("eps", [NP, 2])
        ident = sb("ident", [P, P])
        iota = sb("iota", [P, W])
        ones = sb("ones", [1, P])
        src_all = sb("src_all", [P, NT + SLOTS * T], I32)
        dst_all = sb("dst_all", [P, NT], I32)
        rel = dst_all[:].bitcast(F32)
        idx = sb("idx", [P, SLOTS, T], I32)
        edge = sb("edge", [KE + 1, SLOTS, P])
        rows = sb("rows", [P, SLOTS, T * H])
        msg = sb("msg", [P, T, H + 1])
        hot = sb("hot", [P, T, W])
        sums = sb("sums", [H + 1, N + W])
        lo_p = sb("lo_p", [P, NCH])
        hi_p = sb("hi_p", [P, NCH])
        lo_q = sb("lo_q", [Q, QS])
        hi_q = sb("hi_q", [Q, QS])
        span_q = sb("span_q", [Q, QS], I32)
        shift_q = sb("shift_q", [Q, QS], I32)
        count_q = sb("count_q", [Q, QS])
        lo_row = sb("lo_row", [1, NCH])
        count_row = sb("count_row", [1, NCH])
        zero_row = sb("zero_row", [1, NCH])
        base_tab = sb("base_tab", [1, NCH], I32)
        first_tab = sb("first_tab", [1, NCH + 1], I32)
        agg_in = sb("agg_in", [H + 1, UNITS, UNIT, NP])

        psum = ctx.enter_context(nc.psum_tensor("psum", [P, 8 * BANK], F32))

        def bank(b, n=1):
            return psum[:, b * BANK:(b + n) * BANK]

        ps_hT = bank(0, 2).rearrange("p (i n) -> p i n", n=P)
        ps_out = [bank(2, 3).rearrange("p (i n) -> p i n", n=4 * H), bank(5, 3).rearrange("p (i n) -> p i n", n=4 * H)]
        ps_lo = bank(2, 2).rearrange("p (i n) -> p i n", n=P)
        ps_hi = bank(4, 2).rearrange("p (i n) -> p i n", n=P)
        ps_base = bank(6, 2)
        ps_edge = bank(0)
        ps_seg = bank(1)
        ps_wagg = bank(0)
        ps_upd = [bank(2 + u) for u in range(UNITS)]

        x_landed = [sem(f"x_landed{s}") for s in range(2)]
        w_landed, dst_landed, src_landed = sem("w_landed"), sem("dst_landed"), sem("src_landed")
        table_stored = [sem(f"table_stored{s}") for s in range(2)]
        edge_landed = [sem(f"edge_landed{s}") for s in range(SLOTS)]
        rows_landed = [sem(f"rows_landed{s}") for s in range(SLOTS)]
        ranges_landed, out_stored = sem("ranges_landed"), sem("out_stored")
        filled, consts, w_step, w_scaled = sem("filled"), sem("consts"), sem("w_step"), sem("w_scaled")
        summed, averaged, centred, squared = sem("summed"), sem("averaged"), sem("centred"), sem("squared")
        var_ready, std_ready, rstd_ready, h_ready, r_ready = (
            sem("var_ready"), sem("std_ready"), sem("rstd_ready"), sem("h_ready"), sem("r_ready"))
        turned, turned_copied, node_out, t_copied, q_copied = (
            sem("turned"), sem("turned_copied"), sem("node_out"), sem("t_copied"), sem("q_copied"))
        wagg_ready, wagg_copied = sem("wagg_ready"), sem("wagg_copied")
        ends_ready, ends_turned, range_step, base_spread, tables_ready = (
            sem("ends_ready"), sem("ends_turned"), sem("range_step"), sem("base_spread"), sem("tables_ready"))
        idx_ready, u_ready, z_ready, msg_ready = sem("idx_ready"), sem("u_ready"), sem("z_ready"), sem("msg_ready")
        hot_ready, rel_moved, seg_ready, sums_added = (
            sem("hot_ready"), sem("rel_moved"), sem("seg_ready"), sem("sums_added"))
        agg_copied, upd_ready, y_ready, y_squared, var2_ready, std2_ready, rstd2_ready = (
            sem("agg_copied"), sem("upd_ready"), sem("y_ready"), sem("y_squared"), sem("var2_ready"),
            sem("std2_ready"), sem("rstd2_ready"))
        normed, gelu_ready, result_ready = sem("normed"), sem("gelu_ready"), sem("result_ready")

        weights = [(w3a[0:H, :], w3[0:H, :]), (w3a[H:2 * H, :], w3[0:H, :]), (w3b[:], w3[H:2 * H, :]),
                   (w2b[:, 0:H], w2_t), (w2b[:, H:H + 1], b2.rearrange("(k a) -> k a", a=1)),
                   (w_node[0:H, 0:H], w1[0:H, :]), (w_node[H:2 * H, H:2 * H], w1[0:H, :])]
        for t in range(T):
            weights.append((w_edge[t * D:(t + 1) * D, t * H:(t + 1) * H], w1[H:H + D, :]))
            weights.append((w_edge[KE:KE + 1, t * H:(t + 1) * H], b1.rearrange("(a h) -> a h", a=1)))
        for tile, vec in ((b3_row, b3), (scale_row, ln_scale), (bias_row, ln_bias)):
            weights.append((tile[:], vec.rearrange("(a h) -> a h", a=1).broadcast_to([NP, H])))
        W_LANDED = 16 * len(weights)

        def block_cols(b):
            return bass.ds(b * (BJ * H), BJ * H)

        def unit_cols(g):
            return bass.ds(g * (UNIT * H), UNIT * H)

        def final_cols(i):
            return bass.ds(i * (FJ * H), FJ * H)

        def over_h(vec, n):
            return vec.rearrange("p (j a) -> p j a", a=1).broadcast_to([NP, n, H])

        def over_j(row, n):
            return row.rearrange("p (a h) -> p a h", a=1).broadcast_to([NP, n, H])

        def by_node(cols):
            return cols.rearrange("p (j h) -> p j h", h=H)

        block = ctx.enter_context(nc.Block())

        @block.sync
        def _(sp):
            def load_edges(chunk, k):
                sp.dma_start(edge[0:KE, k, :], edge_t[chunk]).then_inc(edge_landed[k], 16)

            def load_x(b, s):
                for lo, hi in parts:
                    sp.dma_start(xr[lo:hi, block_cols(b)], x_v[lo:hi, block_cols(b)]).then_inc(x_landed[s], 16)

            for s in range(2):
                load_x(s, s)
            with sp.Fori(0, NB // 2 - 1) as i:
                for s in range(2):
                    sp.wait_ge(centred, 2 * i + s + 1)
                    load_x(2 * i + s + 2, s)
            sp.wait_ge(filled, 1)
            for k in range(SLOTS):
                load_edges(k, k)

            with sp.Fori(0, NB // 2) as i:
                for s in range(2):
                    b = 2 * i + s
                    sp.wait_ge(t_copied, b + 1)
                    for lo, hi in parts:
                        sp.dma_start(table_v[lo:hi, block_cols(b)],
                                     t_blk[lo:hi, s, :]).then_inc(table_stored[s], 16)

            sp.wait_ge(range_step, 5)
            sp.dma_start(lo_row[:].rearrange("a (q s) -> a q s", q=Q), lo_q[:]).then_inc(ranges_landed, 16)
            sp.dma_start(count_row[:].rearrange("a (q s) -> a q s", q=Q), count_q[:]).then_inc(ranges_landed, 16)

            with sp.Fori(0, ROUNDS - 1) as i:
                for k in range(SLOTS):
                    c = i * SLOTS + k
                    sp.wait_ge(u_ready, c + 1)
                    load_edges(c + SLOTS, k)

            with sp.Fori(0, FB) as i:
                sp.wait_ge(result_ready, i + 1)
                for lo, hi in parts:
                    sp.dma_start(out_v[lo:hi, final_cols(i)], xr[lo:hi, final_cols(i)]).then_inc(out_stored, 16)
            sp.wait_ge(out_stored, 16 * 2 * FB)

        @block.gpsimd
        def _(pool):
            nc.gpsimd.memset(edge[:], 1.0).then_inc(filled, 1)
            nc.gpsimd.memset(w_edge[:], 0.0).then_inc(filled, 1)
            nc.gpsimd.memset(w_node[:], 0.0).then_inc(filled, 1)
            nc.gpsimd.memset(eps[:, 0:1], LN1_EPS).then_inc(filled, 1)
            nc.gpsimd.memset(eps[:, 1:2], LN2_EPS).then_inc(filled, 1)
            nc.gpsimd.memset(src_all[:, NT:NT + SLOTS * T], 0).then_inc(filled, 1)
            nc.gpsimd.memset(ident[:], 0.0).then_inc(consts, 1)
            pool.wait_ge(consts, 1)
            nc.gpsimd.affine_select(out=ident[:], in_=ident[:], compare_op=ALU.not_equal, fill=1.0, base=0,
                                    pattern=[[-1, P]], channel_multiplier=1).then_inc(consts, 1)
            nc.gpsimd.iota(iota[:], pattern=[[1, W]], base=0, channel_multiplier=0,
                           allow_small_or_imprecise_dtypes=True).then_inc(consts, 1)
            nc.gpsimd.memset(ones[:], 1.0).then_inc(consts, 1)
            nc.gpsimd.memset(zero_row[:], 0.0).then_inc(consts, 1)
            nc.gpsimd.memset(first_tab[:, 0:1], 0).then_inc(consts, 1)
            nc.gpsimd.memset(msg[:, :, H:H + 1], 1.0).then_inc(consts, 1)
            nc.gpsimd.memset(sums[:], 0.0).then_inc(consts, 1)

            with pool.Fori(0, NB // 2) as i:
                for s in range(2):
                    b = 2 * i + s
                    pool.wait_ge(h_ready, b + 1)
                    nc.gpsimd.tensor_tensor(xr[:, block_cols(b)], xr[:, block_cols(b)], h_blk[:, s, :],
                                            ALU.add).then_inc(r_ready, 1)

            for s in range(2):
                pool.wait_ge(table_stored[s], 16 * 2 * (NB // 2))
            with pool.Fori(0, ROUNDS) as i:
                for k in range(SLOTS):
                    c = i * SLOTS + k
                    pool.wait_ge(idx_ready, c + 1)
                    pool.nop(nofuse=True)
                    for t in range(T):
                        nc.gpsimd.indirect_dma_start(
                            out=rows[:, k, t * H:(t + 1) * H], out_offset=None, in_=table,
                            in_offset=bass.IndirectOffsetOnAxis(ap=idx[:, k, t:t + 1], axis=0),
                        ).then_inc(rows_landed[k], 16)

            pool.wait_ge(r_ready, NB)
            with pool.Fori(0, FB) as i:
                pool.wait_ge(gelu_ready, i + 1)
                nc.gpsimd.tensor_tensor(xr[:, final_cols(i)], hq[:, final_cols(i)], xr[:, final_cols(i)],
                                        ALU.add).then_inc(result_ready, 1)

        @block.scalar
        def _(act):
            act.dma_start(dst_all[:], dst_t).then_inc(dst_landed, 16)
            act.dma_start(src_all[:, 0:NT], src_t).then_inc(src_landed, 16)
            act.wait_ge(filled, 3)
            for tile, source in weights:
                act.dma_start(tile, source).then_inc(w_landed, 16)

            with act.Fori(0, NB // 2) as i:
                for s in range(2):
                    b = 2 * i + s
                    act.wait_ge(centred, b + 1)
                    nc.scalar.activation(sq[:, s, :], hq[:, block_cols(b)], ACT.Square).then_inc(squared, 1)
            act.wait_ge(var_ready, NB)
            act.wait_ge(filled, 5)
            nc.scalar.activation(std[:], var[:], ACT.Sqrt, bias=eps[:, 0:1], scale=1.0 / H).then_inc(std_ready, 1)

            act.wait_ge(wagg_ready, 1)
            nc.scalar.copy(w_agg[:], ps_wagg[0:H + 1, 0:H]).then_inc(wagg_copied, 1)

            def node_copies(i, first):
                for s in range(2):
                    b = 2 * i + s
                    act.wait_ge(turned, b + 1)
                    nc.scalar.copy(hT[:, s, :, :], ps_hT[:, 0:PAIRS, 0:NP]).then_inc(turned_copied, 1)
                    act.wait_ge(node_out, b + 1)
                    if not first:
                        act.wait_ge(table_stored[s], 16 * 2 * i)
                    nc.scalar.copy(t_blk[:, s, :].rearrange("p (i n) -> p i n", n=2 * H),
                                   ps_out[s][0:NP, 0:PAIRS, 0:2 * H]).then_inc(t_copied, 1)

            node_copies(0, True)
            with act.Fori(1, NB // 2) as i:
                node_copies(i, False)

            act.wait_ge(src_landed, 16)
            act.wait_ge(filled, 6)
            for k in range(SLOTS):
                nc.scalar.copy(idx[:, k, :], src_all[:, k * T:(k + 1) * T]).then_inc(idx_ready, 1)
            act.wait_ge(consts, 7)
            with act.Fori(0, ROUNDS) as i:
                for k in range(SLOTS):
                    c = i * SLOTS + k
                    act.wait_ge(z_ready, c + 1)
                    nc.scalar.activation(msg[:, :, 0:H], rows[:, k, :].rearrange("p (t h) -> p t h", h=H),
                                         ACT.Gelu_apprx_tanh).then_inc(msg_ready, 1)
                    act.wait_ge(msg_ready, c + 1)
                    nc.scalar.copy(idx[:, k, :], src_all[:, bass.ds((c + SLOTS) * T, T)]).then_inc(idx_ready, 1)

            windows = act.value_load(first_tab[0:1, NCH:NCH + 1], min_val=NCH, max_val=1 << 20)
            act.wait_ge(sums_added, windows)
            sums_v = sums[:, 0:N].rearrange("k (p j) -> k j p", p=NP)

            def update_copies(i, first):
                for u in range(UNITS):
                    g = i * UNITS + u
                    if not first:
                        act.wait_ge(upd_ready, g - UNITS + 1)
                    nc.scalar.copy(agg_in[:, u, :, :], sums_v[:, bass.ds(g * UNIT, UNIT), :]).then_inc(agg_copied, 1)
                act.wait_ge(y_ready, (i + 1) * UNITS)
                nc.scalar.activation(sq[:].rearrange("p s n -> p (s n)"), hq[:, final_cols(i)],
                                     ACT.Square).then_inc(y_squared, 1)

            update_copies(0, True)
            with act.Fori(1, FB) as i:
                update_copies(i, False)
            act.wait_ge(var2_ready, FB)
            nc.scalar.activation(std[:], var[:], ACT.Sqrt, bias=eps[:, 1:2], scale=1.0 / H).then_inc(std2_ready, 1)
            with act.Fori(0, FB) as i:
                act.wait_ge(normed, 3 * i + 3)
                nc.scalar.activation(hq[:, final_cols(i)], hq[:, final_cols(i)],
                                     ACT.Gelu_apprx_tanh).then_inc(gelu_ready, 1)

        @block.tensor
        def _(pe):
            pe.wait_ge(w_step, 6)
            nc.tensor.matmul(ps_wagg[0:H + 1, 0:H], w2b[:], w3bc[:], start=True, stop=True).then_inc(wagg_ready, 1)
            pe.wait_ge(wagg_copied, 1)

            pe.wait_ge(consts, 2)
            pe.wait_ge(w_landed, W_LANDED)

            def node_products(i, first):
                for s in range(2):
                    b = 2 * i + s
                    pe.wait_ge(h_ready, b + 1)
                    for q in range(PAIRS):
                        last = nc.tensor.transpose(ps_hT[:, q, 0:NP], h_blk[:, s, q * 2 * H:(q + 1) * 2 * H],
                                                   ident[0:NP, 0:NP])
                    last.then_inc(turned, 1)
                    pe.wait_ge(turned_copied, b + 1)
                    if not first:
                        pe.wait_ge(t_copied, b - 1)
                        pe.wait_ge(q_copied, b - 1)
                    for q in range(PAIRS):
                        last = nc.tensor.matmul(ps_out[s][0:NP, q, :], hT[:, s, q, :], w_node[:],
                                                start=True, stop=True)
                    last.then_inc(node_out, 1)

            node_products(0, True)
            with pe.Fori(1, NB // 2) as i:
                node_products(i, False)

            pe.wait_ge(t_copied, NB)
            pe.wait_ge(q_copied, NB)
            pe.wait_ge(ends_ready, 2)
            for ends, ps in ((lo_p, ps_lo), (hi_p, ps_hi)):
                by_slot = ends[:].rearrange("p (q s) -> p s q", s=QS)
                for s in range(QS):
                    last = nc.tensor.transpose(ps[0:Q, s, :], by_slot[:, s, :], ident[:])
            last.then_inc(ends_turned, 1)
            pe.wait_ge(ranges_landed, 32)
            pe.wait_ge(consts, 4)
            for n in range(0, NCH, BANK):
                m = min(BANK, NCH - n)
                last = nc.tensor.matmul(ps_base[:, n:n + m], ones[:], lo_row[:, n:n + m], start=True, stop=True)
            last.then_inc(base_spread, 1)

            pe.wait_ge(tables_ready, 1)
            with pe.Fori(0, ROUNDS) as i:
                for k in range(SLOTS):
                    c = i * SLOTS + k
                    pe.wait_ge(edge_landed[k], 16 * i + 16)
                    nc.tensor.matmul(ps_edge[:, 0:T * H], edge[:, k, :], w_edge[:],
                                     start=True, stop=True).then_inc(u_ready, 1)
                    first = pe.value_load(first_tab[0:1, bass.ds(c, 1)], min_val=0, max_val=1 << 20)
                    end = pe.value_load(first_tab[0:1, bass.ds(c + 1, 1)], min_val=1, max_val=1 << 20)
                    with pe.Fori(first, end) as w:
                        pe.wait_ge(msg_ready, c + 1)
                        pe.wait_ge(hot_ready, w + 1)
                        for t in range(T):
                            last = nc.tensor.matmul(ps_seg[0:H + 1, 0:W], msg[:, t, :], hot[:, t, :],
                                                    start=(t == 0), stop=(t == T - 1))
                        last.then_inc(seg_ready, 1)

            def updates(i, first):
                for u in range(UNITS):
                    g = i * UNITS + u
                    pe.wait_ge(agg_copied, g + 1)
                    if not first:
                        pe.wait_ge(y_ready, g - UNITS + 1)
                    for j in range(UNIT):
                        last = nc.tensor.matmul(ps_upd[u][0:NP, j * H:(j + 1) * H], agg_in[:, u, j, :], w_agg[:],
                                                start=True, stop=True)
                    last.then_inc(upd_ready, 1)

            updates(0, True)
            with pe.Fori(1, FB) as i:
                updates(i, False)

        @block.vector
        def _(dve):
            def centre(i, s):
                b = 2 * i + s
                js = bass.ds(b * BJ, BJ)
                dve.wait_ge(x_landed[s], 32 * i + 32)
                nc.vector.tensor_reduce(total[:, js], by_node(xr[:, block_cols(b)]), AX.X, ALU.add).then_inc(summed, 1)
                dve.wait_ge(summed, b + 1)
                nc.vector.tensor_scalar(mean[:, js], total[:, js], 1.0 / H, None, ALU.mult).then_inc(averaged, 1)
                dve.wait_ge(averaged, b + 1)
                nc.vector.tensor_tensor(by_node(hq[:, block_cols(b)]), by_node(xr[:, block_cols(b)]),
                                        over_h(mean[:, js], BJ), ALU.subtract).then_inc(centred, 1)

            with dve.Fori(0, NB // 2) as i:
                for s in range(2):
                    centre(i, s)
                for s in range(2):
                    b = 2 * i + s
                    dve.wait_ge(squared, b + 1)
                    nc.vector.tensor_reduce(var[:, bass.ds(b * BJ, BJ)], by_node(sq[:, s, :]), AX.X,
                                            ALU.add).then_inc(var_ready, 1)

            dve.wait_ge(w_landed, W_LANDED)
            nc.vector.tensor_reduce(wsum[:, 0:1], w3a[:], AX.X, ALU.add).then_inc(w_step, 1)
            nc.vector.tensor_reduce(wsum[0:H, 1:2], w3b[:], AX.X, ALU.add).then_inc(w_step, 1)
            nc.vector.tensor_reduce(wsum[0:NP, 2:3], b3_row[:], AX.X, ALU.add).then_inc(w_step, 1)
            dve.wait_ge(w_step, 3)
            for n, rows_n in enumerate((2 * H, H, NP)):
                sum_n = wsum[0:rows_n, n:n + 1]
                nc.vector.tensor_scalar(sum_n, sum_n, 1.0 / H, None, ALU.mult).then_inc(w_scaled, 1)
            dve.wait_ge(w_scaled, 3)
            nc.vector.tensor_scalar(w3bc[:], w3b[:], wsum[0:H, 1:2], None, ALU.subtract).then_inc(w_step, 1)
            nc.vector.tensor_scalar(b3_c[:], b3_row[:], wsum[0:NP, 2:3], None, ALU.subtract).then_inc(w_step, 1)
            for lo in (0, H):
                last = nc.vector.tensor_scalar(w_node[lo:lo + H, 2 * H + lo:3 * H + lo], w3a[lo:lo + H, :],
                                               wsum[lo:lo + H, 0:1], None, ALU.subtract)
            last.then_inc(w_step, 1)

            dve.wait_ge(std_ready, 1)
            nc.vector.reciprocal(rstd[:], std[:]).then_inc(rstd_ready, 1)
            dve.wait_ge(rstd_ready, 1)

            def node_block(i, first):
                for s in range(2):
                    b = 2 * i + s
                    if not first:
                        dve.wait_ge(turned, b - 1)
                        dve.wait_ge(r_ready, b - 1)
                    nc.vector.scalar_tensor_tensor(
                        out=by_node(h_blk[:, s, :]), in0=by_node(hq[:, block_cols(b)]), scalar=0.0,
                        in1=over_h(rstd[:, bass.ds(b * BJ, BJ)], BJ), op0=ALU.max, op1=ALU.mult).then_inc(h_ready, 1)
                for s in range(2):
                    b = 2 * i + s
                    dve.wait_ge(t_copied, b + 1)
                    for e in range(2):
                        last = nc.vector.tensor_tensor(
                            hq[:, block_cols(b)].rearrange("p (i e h) -> p i e h", e=2, h=H)[:, :, e, :],
                            ps_out[s][0:NP, 0:PAIRS, (2 + e) * H:(3 + e) * H], over_j(b3_c[:], PAIRS), ALU.add)
                    last.then_inc(q_copied, 1)

            node_block(0, True)
            with dve.Fori(1, NB // 2) as i:
                node_block(i, False)

            dve.wait_ge(dst_landed, 16)
            by_chunk = dst_all[:].rearrange("p (c t) -> p c t", t=T)
            nc.vector.tensor_reduce(lo_p[:], by_chunk, AX.X, ALU.min).then_inc(ends_ready, 1)
            nc.vector.tensor_reduce(hi_p[:], by_chunk, AX.X, ALU.max).then_inc(ends_ready, 1)
            dve.wait_ge(ends_turned, 1)
            nc.vector.tensor_reduce(lo_q[:], ps_lo[0:Q, 0:QS, :], AX.X, ALU.min).then_inc(range_step, 1)
            nc.vector.tensor_reduce(hi_q[:], ps_hi[0:Q, 0:QS, :], AX.X, ALU.max).then_inc(range_step, 1)
            dve.wait_ge(range_step, 2)
            nc.vector.tensor_tensor(span_q[:], hi_q[:], lo_q[:], ALU.subtract).then_inc(range_step, 1)
            dve.wait_ge(range_step, 3)
            nc.vector.tensor_scalar(shift_q[:], span_q[:], SHIFT, None, ALU.arith_shift_right).then_inc(range_step, 1)
            dve.wait_ge(range_step, 4)
            nc.vector.tensor_scalar(count_q[:], shift_q[:], 1.0, None, ALU.add).then_inc(range_step, 1)
            dve.wait_ge(ranges_landed, 32)
            dve.wait_ge(consts, 6)
            nc.vector.tensor_copy(base_tab[:], lo_row[:])
            nc.vector.tensor_tensor_scan(first_tab[:, 1:NCH + 1], count_row[:], zero_row[:], 0.0,
                                         ALU.add, ALU.add).then_inc(tables_ready, 1)
            dve.wait_ge(base_spread, 1)
            nc.vector.tensor_tensor(
                rel.rearrange("p (c t) -> p c t", t=T), by_chunk,
                ps_base[:, 0:NCH].rearrange("p (c a) -> p c a", a=1).broadcast_to([P, NCH, T]),
                ALU.subtract).then_inc(tables_ready, 1)
            dve.wait_ge(tables_ready, 2)
            dve.wait_ge(consts, 8)

            iota_t = iota[:].rearrange("p (a w) -> p a w", a=1).broadcast_to([P, T, W])
            with dve.Fori(0, ROUNDS) as i:
                for k in range(SLOTS):
                    c = i * SLOTS + k
                    base = dve.value_load(base_tab[0:1, bass.ds(c, 1)], min_val=0, max_val=N - 1)
                    first = dve.value_load(first_tab[0:1, bass.ds(c, 1)], min_val=0, max_val=1 << 20)
                    end = dve.value_load(first_tab[0:1, bass.ds(c + 1, 1)], min_val=1, max_val=1 << 20)
                    dve.wait_ge(rows_landed[k], 16 * T * i + 16 * T)
                    dve.wait_ge(u_ready, c + 1)
                    nc.vector.tensor_tensor(rows[:, k, :], rows[:, k, :], ps_edge[:, 0:T * H],
                                            ALU.add).then_inc(z_ready, 1)
                    rel_c = rel[:, bass.ds(c * T, T)]
                    with dve.Fori(first, end) as w:
                        nc.vector.tensor_tensor(
                            hot[:], rel_c.rearrange("p (t a) -> p t a", a=1).broadcast_to([P, T, W]), iota_t,
                            ALU.is_equal).then_inc(hot_ready, 1)
                        dve.wait_ge(seg_ready, w + 1)
                        nc.vector.tensor_scalar(rel_c, rel_c, -float(W), None, ALU.add).then_inc(rel_moved, 1)
                        start = nc.s_assert_within(
                            base + (w - first) * W, 0, N - 1,
                            skip_runtime_bounds_check_because="the last window starts at or below the highest dst")
                        window = sums[:, bass.ds(start, W)]
                        nc.vector.tensor_tensor(window, window, ps_seg[0:H + 1, 0:W], ALU.add).then_inc(sums_added, 1)
                        dve.wait_ge(rel_moved, w + 1)

            def update_block(i):
                for u in range(UNITS):
                    g = i * UNITS + u
                    dve.wait_ge(upd_ready, g + 1)
                    nc.vector.tensor_tensor(hq[:, unit_cols(g)], hq[:, unit_cols(g)], ps_upd[u][0:NP, 0:UNIT * H],
                                            ALU.add).then_inc(y_ready, 1)
                dve.wait_ge(y_squared, i + 1)
                nc.vector.tensor_reduce(var[:, bass.ds(i * FJ, FJ)], by_node(sq[:].rearrange("p s n -> p (s n)")),
                                        AX.X, ALU.add).then_inc(var2_ready, 1)

            with dve.Fori(0, FB) as i:
                update_block(i)
            dve.wait_ge(std2_ready, 1)
            nc.vector.reciprocal(rstd[:], std[:]).then_inc(rstd2_ready, 1)
            dve.wait_ge(rstd2_ready, 1)
            with dve.Fori(0, FB) as i:
                y = by_node(hq[:, final_cols(i)])
                nc.vector.tensor_tensor(y, y, over_h(rstd[:, bass.ds(i * FJ, FJ)], FJ), ALU.mult).then_inc(normed, 1)
                dve.wait_ge(normed, 3 * i + 1)
                nc.vector.tensor_tensor(y, y, over_j(scale_row[:], FJ), ALU.mult).then_inc(normed, 1)
                dve.wait_ge(normed, 3 * i + 2)
                nc.vector.tensor_tensor(y, y, over_j(bias_row[:], FJ), ALU.add).then_inc(normed, 1)


_INS = ["x", "src_t", "dst_t", "edge_t", "w1", "b1", "w2_t", "b2", "w3", "b3", "ln_scale", "ln_bias"]


def kernel(x, src, dst, edge_attr_16, L0_gnn_W1, L0_gnn_b1, L0_gnn_W2, L0_gnn_b2, L0_gnn_W3, L0_gnn_b3,
           L0_gnn_ln_scale, L0_gnn_ln_bias):
    import numpy as np
    import concourse.bacc as bacc
    from concourse.bass_utils import run_bass_kernel_spmd

    x, src, dst, edge_attr = (np.asarray(a) for a in (x, src, dst, edge_attr_16))
    E, D = edge_attr.shape
    chunks = E // (T * P)
    laid = {
        "x": x,
        "src_t": src.reshape(E // P, P).T,
        "dst_t": dst.reshape(E // P, P).T,
        "edge_t": edge_attr.reshape(chunks, T, P, D).transpose(0, 1, 3, 2).reshape(chunks, T * D, P),
        "w1": L0_gnn_W1, "b1": L0_gnn_b1, "w2_t": np.asarray(L0_gnn_W2).T, "b2": L0_gnn_b2,
        "w3": L0_gnn_W3, "b3": L0_gnn_b3, "ln_scale": L0_gnn_ln_scale, "ln_bias": L0_gnn_ln_bias,
    }
    nc = bacc.Bacc("TRN2", target_bir_lowering=False, num_devices=1)
    arrays, args = {}, []
    for name in _INS:
        a = np.ascontiguousarray(laid[name])
        arrays[f"in_{name}"] = a
        args.append(nc.dram_tensor(f"in_{name}", a.shape, mybir.dt.from_np(a.dtype), kind="ExternalInput").ap())
    out = nc.dram_tensor("out", x.shape, F32, kind="ExternalOutput").ap()
    gnn_layer(nc, *args, out)
    result = run_bass_kernel_spmd(nc, [arrays], core_ids=[0])
    return result.results[0]["out"]
```

```python
from contextlib import ExitStack

import concourse.bass as bass
from concourse import mybir

F32 = mybir.dt.float32
I32 = mybir.dt.int32
ALU = mybir.AluOpType
ACT = mybir.ActivationFunctionType
AX = mybir.AxisListType

P = 128
T = 5
SLOTS = 5
W = 64
NP = 125
MAIN_P = 120
PAIRS = 5
UNIT = 4
UNITS = 5
BANK = 512
LN1_EPS = 1e-5
LN2_EPS = 1e-6


def gnn_layer(nc, x, src_t, dst_t, edge_t, w1, b1, w2_t, b2, w3, b3, ln_scale, ln_bias, out):
    N, H = x.shape
    NCH, KE, _ = edge_t.shape
    D = KE // T
    NT = NCH * T
    ROUNDS = NCH // SLOTS
    NJ = N // NP
    BJ = 2 * PAIRS
    NB = NJ // BJ
    FJ = UNIT * UNITS
    FB = NJ // FJ
    Q = max(d for d in range(1, P + 1) if NCH % d == 0)
    QS = NCH // Q
    SHIFT = W.bit_length() - 1
    assert NCH % SLOTS == 0 and NJ % (2 * BJ) == 0 and NJ % FJ == 0 and QS <= 8 and NCH <= 2 * BANK

    table = nc.dram_tensor("table", (N, H), F32, kind="Internal").ap()
    x_v = x.rearrange("(p j) h -> p (j h)", p=NP)
    table_v = table.rearrange("(p j) h -> p (j h)", p=NP)
    out_v = out.rearrange("(p j) h -> p (j h)", p=NP)
    parts = [(0, MAIN_P), (MAIN_P, NP)]

    with ExitStack() as ctx:
        def sb(name, shape, dt=F32):
            return ctx.enter_context(nc.sbuf_tensor(name, shape, dt))

        def sem(name):
            return ctx.enter_context(nc.semaphore(name))

        xr = sb("xr", [NP, NJ * H])
        hq = sb("hq", [P, NJ * H])
        h_blk = sb("h_blk", [NP, 2, BJ * H])
        hT = sb("hT", [P, 2, PAIRS, NP])
        t_blk = sb("t_blk", [NP, 2, BJ * H])
        sq = sb("sq", [NP, FJ * H])
        mean = sb("mean", [NP, NJ])
        total = sb("total", [NP, NJ])
        var = sb("var", [NP, NJ])
        std = sb("std", [NP, NJ])
        rstd = sb("rstd", [NP, NJ])
        w_edge = sb("w_edge", [KE + 1, T * H])
        w1_pair = sb("w1_pair", [P, 2 * H])
        w3_pair = sb("w3_pair", [P, 2 * H])
        w3a = sb("w3a", [2 * H, H])
        w3b = sb("w3b", [H, H])
        w3bc = sb("w3bc", [H, H])
        w2b = sb("w2b", [H, H + 1])
        w_agg = sb("w_agg", [H + 1, H])
        wsum = sb("wsum", [P, 4])
        b3_row = sb("b3_row", [NP, H])
        b3_c = sb("b3_c", [NP, H])
        scale_row = sb("scale_row", [NP, H])
        bias_row = sb("bias_row", [NP, H])
        eps = sb("eps", [NP, 2])
        ident = sb("ident", [P, P])
        iota = sb("iota", [P, W])
        ones = sb("ones", [1, P])
        src_all = sb("src_all", [P, NT + SLOTS * T], I32)
        dst_all = sb("dst_all", [P, NT], I32)
        rel = dst_all[:].bitcast(F32)
        idx = sb("idx", [P, SLOTS, T], I32)
        edge = sb("edge", [KE + 1, SLOTS, P])
        rows = sb("rows", [P, SLOTS, T * H])
        msg = sb("msg", [P, T, H + 1])
        hot = sb("hot", [P, T, W])
        sums = sb("sums", [H + 1, N + W])
        lo_p = sb("lo_p", [P, NCH])
        hi_p = sb("hi_p", [P, NCH])
        lo_q = sb("lo_q", [Q, QS])
        hi_q = sb("hi_q", [Q, QS])
        span_q = sb("span_q", [Q, QS], I32)
        shift_q = sb("shift_q", [Q, QS], I32)
        count_q = sb("count_q", [Q, QS])
        lo_row = sb("lo_row", [1, NCH])
        count_row = sb("count_row", [1, NCH])
        zero_row = sb("zero_row", [1, NCH])
        base_tab = sb("base_tab", [1, NCH], I32)
        first_tab = sb("first_tab", [1, NCH + 1], I32)
        agg_in = sb("agg_in", [H + 1, UNITS, UNIT, NP])

        psum = ctx.enter_context(nc.psum_tensor("psum", [P, 8 * BANK], F32))

        def bank(b, n=1):
            return psum[:, b * BANK:(b + n) * BANK]

        ps_hT = [bank(2 * s, 2).rearrange("p (i n) -> p i n", n=P) for s in range(2)]
        ps_out = [bank(4 + 2 * s, 2) for s in range(2)]
        ps_base = bank(2, 2)
        ps_lo = bank(4, 2).rearrange("p (i n) -> p i n", n=P)
        ps_hi = bank(6, 2).rearrange("p (i n) -> p i n", n=P)
        ps_edge = bank(0)
        ps_seg = bank(1)
        ps_q = bank(2, 2)
        ps_wagg = bank(1)
        ps_upd = [bank(2 + u) for u in range(UNITS)]

        x_landed = [sem(f"x_landed{s}") for s in range(FB)]
        w_landed, dst_landed, src_landed = sem("w_landed"), sem("dst_landed"), sem("src_landed")
        table_stored = [sem(f"table_stored{s}") for s in range(2)]
        edge_landed = [sem(f"edge_landed{s}") for s in range(SLOTS)]
        rows_landed = [sem(f"rows_landed{s}") for s in range(SLOTS)]
        ranges_landed, out_stored = sem("ranges_landed"), sem("out_stored")
        filled, consts, w_step, w_scaled = sem("filled"), sem("consts"), sem("w_step"), sem("w_scaled")
        summed, averaged, centred, squared, var_ready, std_ready, rstd_ready = (
            sem("summed"), sem("averaged"), sem("centred"), sem("squared"), sem("var_ready"), sem("std_ready"),
            sem("rstd_ready"))
        h_ready, r_ready = sem("h_ready"), sem("r_ready")
        turned, turned_copied, node_out, t_copied = (
            sem("turned"), sem("turned_copied"), sem("node_out"), sem("t_copied"))
        hT_saved = [sem(f"hT_saved{s}") for s in range(2)]
        hT_back, q_out, q_ready = sem("hT_back"), sem("q_out"), sem("q_ready")
        wagg_ready, wagg_copied = sem("wagg_ready"), sem("wagg_copied")
        ends_ready, ends_turned, range_step, base_spread, tables_ready = (
            sem("ends_ready"), sem("ends_turned"), sem("range_step"), sem("base_spread"), sem("tables_ready"))
        idx_ready, u_ready, z_ready, msg_ready = sem("idx_ready"), sem("u_ready"), sem("z_ready"), sem("msg_ready")
        sums_zero = sem("sums_zero")
        hot_ready, rel_moved, seg_ready, sums_added = (
            sem("hot_ready"), sem("rel_moved"), sem("seg_ready"), sem("sums_added"))
        agg_copied, upd_ready, y_ready, y_squared, var2_ready, std2_ready, rstd2_ready = (
            sem("agg_copied"), sem("upd_ready"), sem("y_ready"), sem("y_squared"), sem("var2_ready"),
            sem("std2_ready"), sem("rstd2_ready"))
        normed, gelu_ready, result_ready = sem("normed"), sem("gelu_ready"), sem("result_ready")

        weights = [(w3a[0:H, :], w3[0:H, :]), (w3a[H:2 * H, :], w3[0:H, :]), (w3b[:], w3[H:2 * H, :]),
                   (w2b[:, 0:H], w2_t), (w2b[:, H:H + 1], b2.rearrange("(k a) -> k a", a=1)),
                   (w1_pair[0:H, 0:H], w1[0:H, :]), (w1_pair[H:2 * H, H:2 * H], w1[0:H, :]),
                   (w_edge[KE:KE + 1, :].rearrange("a (t h) -> a t h", t=T),
                    b1.rearrange("(a t h) -> a t h", a=1, t=1).broadcast_to([1, T, H]))]
        for t in range(T):
            weights.append((w_edge[t * D:(t + 1) * D, t * H:(t + 1) * H], w1[H:H + D, :]))
        for tile, vec in ((b3_row, b3), (scale_row, ln_scale), (bias_row, ln_bias)):
            weights.append((tile[:], vec.rearrange("(a h) -> a h", a=1).broadcast_to([NP, H])))
        W_LANDED = 16 * len(weights)

        def block_cols(b):
            return bass.ds(b * (BJ * H), BJ * H)

        def saved_cols(b):
            return bass.ds(b * (PAIRS * NP), PAIRS * NP)

        def unit_cols(g):
            return bass.ds(g * (UNIT * H), UNIT * H)

        def final_cols(i):
            return bass.ds(i * (FJ * H), FJ * H)

        def over_h(vec, n):
            return vec.rearrange("p (j a) -> p j a", a=1).broadcast_to([NP, n, H])

        def over_j(row, n):
            return row.rearrange("p (a h) -> p a h", a=1).broadcast_to([NP, n, H])

        def by_node(cols):
            return cols.rearrange("p (j h) -> p j h", h=H)

        squares_at = (sq[:], h_blk[:].rearrange("p s n -> p (s n)"))

        block = ctx.enter_context(nc.Block())

        @block.sync
        def _(sp):
            def load_edges(chunk, k):
                sp.dma_start(edge[0:KE, k, :], edge_t[chunk]).then_inc(edge_landed[k], 16)

            for g in range(FB):
                for lo, hi in parts:
                    sp.dma_start(xr[lo:hi, final_cols(g)], x_v[lo:hi, final_cols(g)]).then_inc(x_landed[g], 16)
            sp.wait_ge(filled, 3)
            for tile, source in weights:
                sp.dma_start(tile, source).then_inc(w_landed, 16)
            sp.dma_start(src_all[:, 0:NT], src_t).then_inc(src_landed, 16)
            sp.dma_start(dst_all[:], dst_t).then_inc(dst_landed, 16)
            for k in range(SLOTS):
                load_edges(k, k)

            with sp.Fori(0, NB // 2) as i:
                for s in range(2):
                    b = 2 * i + s
                    sp.wait_ge(turned_copied, b + 1)
                    sp.dma_start(hq[:, saved_cols(b)], hT[:, s, :, :].rearrange("p i n -> p (i n)")).then_inc(hT_saved[s], 16)
                    sp.wait_ge(t_copied, b + 1)
                    for lo, hi in parts:
                        sp.dma_start(table_v[lo:hi, block_cols(b)],
                                     t_blk[lo:hi, s, :]).then_inc(table_stored[s], 16)

            sp.wait_ge(range_step, 5)
            sp.dma_start(lo_row[:].rearrange("a (q s) -> a q s", q=Q), lo_q[:]).then_inc(ranges_landed, 16)
            sp.dma_start(count_row[:].rearrange("a (q s) -> a q s", q=Q), count_q[:]).then_inc(ranges_landed, 16)

            def next_edges(i):
                for k in range(SLOTS):
                    c = i * SLOTS + k
                    sp.wait_ge(u_ready, c + 1)
                    load_edges(c + SLOTS, k)

            def hT_again(cols):
                sp.dma_start(hT[:, 0, :, :].rearrange("p i n -> p (i n)"), hq[:, cols]).then_inc(hT_back, 16)

            for s in range(2):
                sp.wait_ge(hT_saved[s], 16 * (NB // 2))
            sp.wait_ge(node_out, NB)
            hT_again(saved_cols(NB - 1))
            next_edges(0)
            with sp.Fori(1, NB) as i:
                cols = bass.ds(sp.snap(i * -(PAIRS * NP) + (NB - 1) * PAIRS * NP), PAIRS * NP)
                sp.wait_ge(q_ready, i)
                hT_again(cols)
                next_edges(i)
            with sp.Fori(NB, ROUNDS - 1) as i:
                next_edges(i)

            with sp.Fori(0, FB) as i:
                sp.wait_ge(result_ready, i + 1)
                for lo, hi in parts:
                    sp.dma_start(out_v[lo:hi, final_cols(i)], xr[lo:hi, final_cols(i)]).then_inc(out_stored, 16)
            sp.wait_ge(out_stored, 16 * 2 * FB)

        @block.gpsimd
        def _(pool):
            nc.gpsimd.memset(edge[:], 1.0).then_inc(filled, 1)
            nc.gpsimd.memset(w_edge[:], 0.0).then_inc(filled, 1)
            nc.gpsimd.memset(w1_pair[:], 0.0).then_inc(filled, 1)
            nc.gpsimd.memset(eps[:, 0:1], LN1_EPS).then_inc(filled, 1)
            nc.gpsimd.memset(eps[:, 1:2], LN2_EPS).then_inc(filled, 1)
            nc.gpsimd.memset(src_all[:, NT:NT + SLOTS * T], 0).then_inc(filled, 1)
            nc.gpsimd.memset(w3_pair[:], 0.0).then_inc(filled, 1)
            nc.gpsimd.memset(ident[:], 0.0).then_inc(consts, 1)
            pool.wait_ge(consts, 1)
            nc.gpsimd.affine_select(out=ident[:], in_=ident[:], compare_op=ALU.not_equal, fill=1.0, base=0,
                                    pattern=[[-1, P]], channel_multiplier=1).then_inc(consts, 1)
            nc.gpsimd.iota(iota[:], pattern=[[1, W]], base=0, channel_multiplier=0,
                           allow_small_or_imprecise_dtypes=True).then_inc(consts, 1)
            nc.gpsimd.memset(ones[:], 1.0).then_inc(consts, 1)
            nc.gpsimd.memset(zero_row[:], 0.0).then_inc(consts, 1)
            nc.gpsimd.memset(first_tab[:, 0:1], 0).then_inc(consts, 1)
            nc.gpsimd.memset(msg[:, :, H:H + 1], 1.0).then_inc(consts, 1)

            for g in range(FB):
                pool.wait_ge(averaged, g + 1)
                nc.gpsimd.tensor_tensor(by_node(hq[0:NP, final_cols(g)]), by_node(xr[:, final_cols(g)]),
                                        over_h(mean[:, g * FJ:(g + 1) * FJ], FJ), ALU.subtract).then_inc(centred, 1)

            with pool.Fori(0, NB // 2) as i:
                for s in range(2):
                    b = 2 * i + s
                    pool.wait_ge(h_ready, b + 1)
                    nc.gpsimd.tensor_tensor(xr[:, block_cols(b)], xr[:, block_cols(b)], h_blk[:, s, :],
                                            ALU.add).then_inc(r_ready, 1)

            for s in range(2):
                pool.wait_ge(table_stored[s], 16 * 2 * (NB // 2))
            with pool.Fori(0, ROUNDS) as i:
                for k in range(SLOTS):
                    c = i * SLOTS + k
                    pool.wait_ge(idx_ready, c + 1)
                    pool.nop(nofuse=True)
                    for t in range(T):
                        nc.gpsimd.indirect_dma_start(
                            out=rows[:, k, t * H:(t + 1) * H], out_offset=None, in_=table,
                            in_offset=bass.IndirectOffsetOnAxis(ap=idx[:, k, t:t + 1], axis=0),
                        ).then_inc(rows_landed[k], 16)

            pool.wait_ge(r_ready, NB)
            with pool.Fori(0, FB) as i:
                pool.wait_ge(gelu_ready, i + 1)
                nc.gpsimd.tensor_tensor(xr[:, final_cols(i)], hq[0:NP, final_cols(i)], xr[:, final_cols(i)],
                                        ALU.add).then_inc(result_ready, 1)

        @block.scalar
        def _(act):
            for g in range(FB):
                act.wait_ge(centred, g + 1)
                if g >= 2:
                    act.wait_ge(var_ready, g - 1)
                nc.scalar.activation(squares_at[g % 2], hq[0:NP, final_cols(g)], ACT.Square).then_inc(squared, 1)
            act.wait_ge(var_ready, FB)
            act.wait_ge(filled, 5)
            nc.scalar.activation(std[:], var[:], ACT.Sqrt, bias=eps[:, 0:1], scale=1.0 / H).then_inc(std_ready, 1)

            def copy_turned(i, s, first):
                act.wait_ge(turned, 2 * i + s + 1)
                if not first:
                    act.wait_ge(node_out, 2 * i + s - 1)
                    act.wait_ge(hT_saved[s], 16 * i)
                nc.scalar.copy(hT[:, s, :, :], ps_hT[s][:, 0:PAIRS, 0:NP]).then_inc(turned_copied, 1)

            def copy_products(i, s, first):
                act.wait_ge(node_out, 2 * i + s + 1)
                if not first:
                    act.wait_ge(table_stored[s], 32 * i)
                nc.scalar.copy(t_blk[:, s, :], ps_out[s][0:NP, 0:BJ * H]).then_inc(t_copied, 1)

            def node_copies(i, first, last):
                copy_turned(i, 1, first)
                copy_products(i, 0, first)
                if not last:
                    copy_turned(i + 1, 0, False)
                copy_products(i, 1, first)

            copy_turned(0, 0, True)
            node_copies(0, True, False)
            with act.Fori(1, NB // 2 - 1) as i:
                node_copies(i, False, False)
            node_copies(NB // 2 - 1, False, True)

            act.wait_ge(src_landed, 16)
            act.wait_ge(filled, 6)
            for k in range(SLOTS):
                nc.scalar.copy(idx[:, k, :], src_all[:, k * T:(k + 1) * T]).then_inc(idx_ready, 1)
            act.wait_ge(wagg_ready, 1)
            nc.scalar.copy(w_agg[:], ps_wagg[0:H + 1, 0:H]).then_inc(wagg_copied, 1)

            act.wait_ge(consts, 7)
            with act.Fori(0, ROUNDS) as i:
                for k in range(SLOTS):
                    c = i * SLOTS + k
                    act.wait_ge(z_ready, c + 1)
                    nc.scalar.activation(msg[:, :, 0:H], rows[:, k, :].rearrange("p (t h) -> p t h", h=H),
                                         ACT.Gelu_apprx_tanh).then_inc(msg_ready, 1)
                    act.wait_ge(msg_ready, c + 1)
                    nc.scalar.copy(idx[:, k, :], src_all[:, bass.ds((c + SLOTS) * T, T)]).then_inc(idx_ready, 1)

            windows = act.value_load(first_tab[0:1, NCH:NCH + 1], min_val=NCH, max_val=1 << 20)
            act.wait_ge(sums_added, windows)
            sums_v = sums[:, 0:N].rearrange("k (p j) -> k j p", p=NP)

            def update_copies(i):
                for u in range(UNITS):
                    g = i * UNITS + u
                    if i:
                        act.wait_ge(upd_ready, g - UNITS + 1)
                    nc.scalar.copy(agg_in[:, u, :, :], sums_v[:, g * UNIT:(g + 1) * UNIT, :]).then_inc(agg_copied, 1)

            update_copies(0)
            for i in range(FB + 2):
                if i + 1 < FB:
                    update_copies(i + 1)
                if i < FB:
                    act.wait_ge(y_ready, (i + 1) * UNITS)
                    if i:
                        act.wait_ge(var2_ready, i)
                    nc.scalar.activation(sq[:], hq[0:NP, final_cols(i)], ACT.Square).then_inc(y_squared, 1)
                    act.wait_ge(var2_ready, i + 1)
                    js = slice(i * FJ, (i + 1) * FJ)
                    nc.scalar.activation(std[:, js], var[:, js], ACT.Sqrt, bias=eps[:, 1:2],
                                         scale=1.0 / H).then_inc(std2_ready, 1)
                if i >= 2:
                    act.wait_ge(normed, 3 * (i - 1))
                    nc.scalar.activation(hq[0:NP, final_cols(i - 2)], hq[0:NP, final_cols(i - 2)],
                                         ACT.Gelu_apprx_tanh).then_inc(gelu_ready, 1)

        @block.tensor
        def _(pe):
            pe.wait_ge(consts, 2)
            pe.wait_ge(w_landed, W_LANDED)

            def turn(b, s):
                pe.wait_ge(h_ready, b + 1)
                for q in range(PAIRS):
                    last = nc.tensor.transpose(ps_hT[s][:, q, 0:NP], h_blk[:, s, q * 2 * H:(q + 1) * 2 * H],
                                               ident[0:NP, 0:NP])
                last.then_inc(turned, 1)

            def products(b, s, first):
                pe.wait_ge(turned_copied, b + 1)
                if not first:
                    pe.wait_ge(t_copied, b - 1)
                for q in range(PAIRS):
                    last = nc.tensor.matmul(ps_out[s][0:NP, q * 2 * H:(q + 1) * 2 * H], hT[:, s, q, :], w1_pair[:],
                                            start=True, stop=True)
                last.then_inc(node_out, 1)

            def node_pair(i, first, last):
                turn(2 * i + 1, 1)
                products(2 * i, 0, first)
                if not last:
                    turn(2 * i + 2, 0)
                products(2 * i + 1, 1, first)

            turn(0, 0)
            node_pair(0, True, False)
            with pe.Fori(1, NB // 2 - 1) as i:
                node_pair(i, False, False)
            node_pair(NB // 2 - 1, False, True)

            pe.wait_ge(t_copied, NB)
            pe.wait_ge(ends_ready, 2)
            for ends, ps in ((lo_p, ps_lo), (hi_p, ps_hi)):
                by_slot = ends[:].rearrange("p (q s) -> p s q", s=QS)
                for s in range(QS):
                    last = nc.tensor.transpose(ps[0:Q, s, :], by_slot[:, s, :], ident[:])
            last.then_inc(ends_turned, 1)
            pe.wait_ge(w_step, 6)
            nc.tensor.matmul(ps_wagg[0:H + 1, 0:H], w2b[:], w3bc[:], start=True, stop=True).then_inc(wagg_ready, 1)
            pe.wait_ge(ranges_landed, 32)
            pe.wait_ge(consts, 4)
            for n in range(0, NCH, BANK):
                m = min(BANK, NCH - n)
                last = nc.tensor.matmul(ps_base[:, n:n + m], ones[:], lo_row[:, n:n + m], start=True, stop=True)
            last.then_inc(base_spread, 1)

            pe.wait_ge(tables_ready, 2)
            pe.wait_ge(wagg_copied, 1)

            def edge_chunk(i, k):
                c = i * SLOTS + k
                pe.wait_ge(edge_landed[k], 16 * i + 16)
                nc.tensor.matmul(ps_edge[:, 0:T * H], edge[:, k, :], w_edge[:], start=True, stop=True).then_inc(u_ready, 1)
                first = pe.value_load(first_tab[0:1, bass.ds(c, 1)], min_val=0, max_val=1 << 20)
                end = pe.value_load(first_tab[0:1, bass.ds(c + 1, 1)], min_val=1, max_val=1 << 20)
                with pe.Fori(first, end) as w:
                    pe.wait_ge(msg_ready, c + 1)
                    pe.wait_ge(hot_ready, w + 1)
                    for t in range(T):
                        last = nc.tensor.matmul(ps_seg[0:H + 1, 0:W], msg[:, t, :], hot[:, t, :],
                                                start=(t == 0), stop=(t == T - 1))
                    last.then_inc(seg_ready, 1)

            with pe.Fori(0, NB) as i:
                for k in range(SLOTS):
                    edge_chunk(i, k)
                    if k == 1:
                        pe.wait_ge(hT_back, 16 * i + 16)
                        for q in range(PAIRS):
                            last = nc.tensor.matmul(ps_q[0:NP, q * 2 * H:(q + 1) * 2 * H], hT[:, 0, q, :], w3_pair[:],
                                                    start=True, stop=True)
                        last.then_inc(q_out, 1)
            with pe.Fori(NB, ROUNDS) as i:
                for k in range(SLOTS):
                    edge_chunk(i, k)

            def updates(i, first):
                for u in range(UNITS):
                    g = i * UNITS + u
                    pe.wait_ge(agg_copied, g + 1)
                    if not first:
                        pe.wait_ge(y_ready, g - UNITS + 1)
                    for j in range(UNIT):
                        last = nc.tensor.matmul(ps_upd[u][0:NP, j * H:(j + 1) * H], agg_in[:, u, j, :], w_agg[:],
                                                start=True, stop=True)
                    last.then_inc(upd_ready, 1)

            updates(0, True)
            with pe.Fori(1, FB) as i:
                updates(i, False)

        @block.vector
        def _(dve):
            def sum_x_squares(g):
                dve.wait_ge(squared, g + 1)
                nc.vector.tensor_reduce(var[:, g * FJ:(g + 1) * FJ], by_node(squares_at[g % 2]), AX.X,
                                        ALU.add).then_inc(var_ready, 1)

            for g in range(FB):
                js = slice(g * FJ, (g + 1) * FJ)
                dve.wait_ge(x_landed[g], 32)
                nc.vector.tensor_reduce(total[:, js], by_node(xr[:, final_cols(g)]), AX.X, ALU.add).then_inc(summed, 1)
                dve.wait_ge(summed, g + 1)
                nc.vector.tensor_scalar(mean[:, js], total[:, js], 1.0 / H, None, ALU.mult).then_inc(averaged, 1)
                if g >= 2:
                    sum_x_squares(g - 2)
            for g in range(FB - 2, FB):
                sum_x_squares(g)

            dve.wait_ge(std_ready, 1)
            nc.vector.reciprocal(rstd[:], std[:]).then_inc(rstd_ready, 1)
            dve.wait_ge(rstd_ready, 1)

            def node_block(i, first):
                for s in range(2):
                    b = 2 * i + s
                    if not first:
                        dve.wait_ge(turned, b - 1)
                        dve.wait_ge(r_ready, b - 1)
                    nc.vector.scalar_tensor_tensor(
                        out=by_node(h_blk[:, s, :]), in0=by_node(hq[0:NP, block_cols(b)]), scalar=0.0,
                        in1=over_h(rstd[:, bass.ds(b * BJ, BJ)], BJ), op0=ALU.max, op1=ALU.mult).then_inc(h_ready, 1)

            node_block(0, True)
            with dve.Fori(1, NB // 2) as i:
                node_block(i, False)

            dve.wait_ge(dst_landed, 16)
            by_chunk = dst_all[:].rearrange("p (c t) -> p c t", t=T)
            nc.vector.tensor_reduce(lo_p[:], by_chunk, AX.X, ALU.min).then_inc(ends_ready, 1)
            nc.vector.tensor_reduce(hi_p[:], by_chunk, AX.X, ALU.max).then_inc(ends_ready, 1)
            dve.wait_ge(w_landed, W_LANDED)
            dve.wait_ge(filled, 7)
            nc.vector.tensor_reduce(wsum[:, 0:1], w3a[:], AX.X, ALU.add).then_inc(w_step, 1)
            nc.vector.tensor_reduce(wsum[0:H, 1:2], w3b[:], AX.X, ALU.add).then_inc(w_step, 1)
            nc.vector.tensor_reduce(wsum[0:NP, 2:3], b3_row[:], AX.X, ALU.add).then_inc(w_step, 1)
            dve.wait_ge(w_step, 3)
            for n, rows_n in enumerate((2 * H, H, NP)):
                sum_n = wsum[0:rows_n, n:n + 1]
                nc.vector.tensor_scalar(sum_n, sum_n, 1.0 / H, None, ALU.mult).then_inc(w_scaled, 1)
            dve.wait_ge(w_scaled, 3)
            nc.vector.tensor_scalar(w3bc[:], w3b[:], wsum[0:H, 1:2], None, ALU.subtract).then_inc(w_step, 1)
            nc.vector.tensor_scalar(b3_c[:], b3_row[:], wsum[0:NP, 2:3], None, ALU.subtract).then_inc(w_step, 1)
            for lo in (0, H):
                last = nc.vector.tensor_scalar(w3_pair[lo:lo + H, lo:lo + H], w3a[lo:lo + H, :],
                                               wsum[lo:lo + H, 0:1], None, ALU.subtract)
            last.then_inc(w_step, 1)

            dve.wait_ge(ends_turned, 1)
            nc.vector.tensor_reduce(lo_q[:], ps_lo[0:Q, 0:QS, :], AX.X, ALU.min).then_inc(range_step, 1)
            nc.vector.tensor_reduce(hi_q[:], ps_hi[0:Q, 0:QS, :], AX.X, ALU.max).then_inc(range_step, 1)
            dve.wait_ge(range_step, 2)
            nc.vector.tensor_tensor(span_q[:], hi_q[:], lo_q[:], ALU.subtract).then_inc(range_step, 1)
            dve.wait_ge(range_step, 3)
            nc.vector.tensor_scalar(shift_q[:], span_q[:], SHIFT, None, ALU.arith_shift_right).then_inc(range_step, 1)
            dve.wait_ge(range_step, 4)
            nc.vector.tensor_scalar(count_q[:], shift_q[:], 1.0, None, ALU.add).then_inc(range_step, 1)
            nc.vector.memset(sums[:], 0.0).then_inc(sums_zero, 1)
            dve.wait_ge(ranges_landed, 32)
            dve.wait_ge(consts, 6)
            nc.vector.tensor_copy(base_tab[:], lo_row[:])
            nc.vector.tensor_tensor_scan(first_tab[:, 1:NCH + 1], count_row[:], zero_row[:], 0.0,
                                         ALU.add, ALU.add).then_inc(tables_ready, 1)
            dve.wait_ge(base_spread, 1)
            nc.vector.tensor_tensor(
                rel.rearrange("p (c t) -> p c t", t=T), by_chunk,
                ps_base[:, 0:NCH].rearrange("p (c a) -> p c a", a=1).broadcast_to([P, NCH, T]),
                ALU.subtract).then_inc(tables_ready, 1)
            dve.wait_ge(tables_ready, 2)
            dve.wait_ge(sums_zero, 1)
            dve.wait_ge(consts, 3)

            iota_t = iota[:].rearrange("p (a w) -> p a w", a=1).broadcast_to([P, T, W])
            def edge_chunk(i, k):
                c = i * SLOTS + k
                base = dve.value_load(base_tab[0:1, bass.ds(c, 1)], min_val=0, max_val=N - 1)
                first = dve.value_load(first_tab[0:1, bass.ds(c, 1)], min_val=0, max_val=1 << 20)
                end = dve.value_load(first_tab[0:1, bass.ds(c + 1, 1)], min_val=1, max_val=1 << 20)
                dve.wait_ge(rows_landed[k], 16 * T * i + 16 * T)
                dve.wait_ge(u_ready, c + 1)
                nc.vector.tensor_tensor(rows[:, k, :], rows[:, k, :], ps_edge[:, 0:T * H],
                                        ALU.add).then_inc(z_ready, 1)
                rel_c = rel[:, bass.ds(c * T, T)]
                with dve.Fori(first, end) as w:
                    nc.vector.tensor_tensor(
                        hot[:], rel_c.rearrange("p (t a) -> p t a", a=1).broadcast_to([P, T, W]), iota_t,
                        ALU.is_equal).then_inc(hot_ready, 1)
                    dve.wait_ge(seg_ready, w + 1)
                    nc.vector.tensor_scalar(rel_c, rel_c, -float(W), None, ALU.add).then_inc(rel_moved, 1)
                    start = nc.s_assert_within(
                        base + (w - first) * W, 0, N - 1,
                        skip_runtime_bounds_check_because="the last window starts at or below the highest dst")
                    window = sums[:, bass.ds(start, W)]
                    nc.vector.tensor_tensor(window, window, ps_seg[0:H + 1, 0:W], ALU.add).then_inc(sums_added, 1)
                    dve.wait_ge(rel_moved, w + 1)

            with dve.Fori(0, NB) as i:
                cols = bass.ds(dve.snap(i * -(BJ * H) + (NB - 1) * BJ * H), BJ * H)
                for k in range(SLOTS):
                    edge_chunk(i, k)
                    if k == 2:
                        dve.wait_ge(q_out, i + 1)
                        nc.vector.tensor_tensor(by_node(hq[0:NP, cols]), by_node(ps_q[0:NP, 0:BJ * H]),
                                                over_j(b3_c[:], BJ), ALU.add).then_inc(q_ready, 1)
            with dve.Fori(NB, ROUNDS) as i:
                for k in range(SLOTS):
                    edge_chunk(i, k)

            dve.wait_ge(q_ready, NB)

            def add_updates(i):
                for u in range(UNITS):
                    g = i * UNITS + u
                    dve.wait_ge(upd_ready, g + 1)
                    nc.vector.tensor_tensor(hq[0:NP, unit_cols(g)], hq[0:NP, unit_cols(g)], ps_upd[u][0:NP, 0:UNIT * H],
                                            ALU.add).then_inc(y_ready, 1)

            for i in range(FB + 1):
                if i < FB:
                    add_updates(i)
                    dve.wait_ge(y_squared, i + 1)
                    nc.vector.tensor_reduce(var[:, i * FJ:(i + 1) * FJ], by_node(sq[:]), AX.X,
                                            ALU.add).then_inc(var2_ready, 1)
                if i:
                    js = slice((i - 1) * FJ, i * FJ)
                    y = by_node(hq[0:NP, final_cols(i - 1)])
                    dve.wait_ge(std2_ready, i)
                    nc.vector.reciprocal(rstd[:, js], std[:, js]).then_inc(rstd2_ready, 1)
                    dve.wait_ge(rstd2_ready, i)
                    nc.vector.tensor_tensor(y, y, over_h(rstd[:, js], FJ), ALU.mult).then_inc(normed, 1)
                    dve.wait_ge(normed, 3 * i - 2)
                    nc.vector.tensor_tensor(y, y, over_j(scale_row[:], FJ), ALU.mult).then_inc(normed, 1)
                    dve.wait_ge(normed, 3 * i - 1)
                    nc.vector.tensor_tensor(y, y, over_j(bias_row[:], FJ), ALU.add).then_inc(normed, 1)


_INS = ["x", "src_t", "dst_t", "edge_t", "w1", "b1", "w2_t", "b2", "w3", "b3", "ln_scale", "ln_bias"]


def kernel(x, src, dst, edge_attr_16, L0_gnn_W1, L0_gnn_b1, L0_gnn_W2, L0_gnn_b2, L0_gnn_W3, L0_gnn_b3,
           L0_gnn_ln_scale, L0_gnn_ln_bias):
    import numpy as np
    import concourse.bacc as bacc
    from concourse.bass_utils import run_bass_kernel_spmd

    x, src, dst, edge_attr = (np.asarray(a) for a in (x, src, dst, edge_attr_16))
    E, D = edge_attr.shape
    chunks = E // (T * P)
    laid = {
        "x": x,
        "src_t": src.reshape(E // P, P).T,
        "dst_t": dst.reshape(E // P, P).T,
        "edge_t": edge_attr.reshape(chunks, T, P, D).transpose(0, 1, 3, 2).reshape(chunks, T * D, P),
        "w1": L0_gnn_W1, "b1": L0_gnn_b1, "w2_t": np.asarray(L0_gnn_W2).T, "b2": L0_gnn_b2,
        "w3": L0_gnn_W3, "b3": L0_gnn_b3, "ln_scale": L0_gnn_ln_scale, "ln_bias": L0_gnn_ln_bias,
    }
    nc = bacc.Bacc("TRN2", target_bir_lowering=False, num_devices=1)
    arrays, args = {}, []
    for name in _INS:
        a = np.ascontiguousarray(laid[name])
        arrays[f"in_{name}"] = a
        args.append(nc.dram_tensor(f"in_{name}", a.shape, mybir.dt.from_np(a.dtype), kind="ExternalInput").ap())
    out = nc.dram_tensor("out", x.shape, F32, kind="ExternalOutput").ap()
    gnn_layer(nc, *args, out)
    result = run_bass_kernel_spmd(nc, [arrays], core_ids=[0])
    return result.results[0]["out"]
```

```python
from contextlib import ExitStack

import concourse.bass as bass
from concourse import mybir

F32 = mybir.dt.float32
I32 = mybir.dt.int32
ALU = mybir.AluOpType
ACT = mybir.ActivationFunctionType
AX = mybir.AxisListType

P = 128
T = 5
SLOTS = 5
RAW = 10
W = 64
NP = 125
MAIN_P = 120
PAIRS = 5
UNIT = 4
UNITS = 5
BANK = 512
LN1_EPS = 1e-5
LN2_EPS = 1e-6


def gnn_layer(nc, x, src_t, dst_t, edge_t, w1, b1, w2_t, b2, w3, b3, ln_scale, ln_bias, out):
    N, H = x.shape
    NCH, KE, _ = edge_t.shape
    D = KE // T
    NT = NCH * T
    MIX = SLOTS + 1
    ROUNDS = RAW + (NCH - MIX * RAW) // SLOTS
    NJ = N // NP
    BJ = 2 * PAIRS
    NB = NJ // BJ
    FJ = UNIT * UNITS
    FB = NJ // FJ
    Q = max(d for d in range(1, P + 1) if NCH % d == 0)
    QS = NCH // Q
    SHIFT = W.bit_length() - 1
    assert (NCH - MIX * RAW) % SLOTS == 0 and ROUNDS > RAW + NB + 1 and NJ % (2 * BJ) == 0 and NJ % FJ == 0 and QS <= 8 and NCH <= 2 * BANK

    table = nc.dram_tensor("table", (N, H), F32, kind="Internal").ap()
    x_v = x.rearrange("(p j) h -> p (j h)", p=NP)
    table_v = table.rearrange("(p j) h -> p (j h)", p=NP)
    out_v = out.rearrange("(p j) h -> p (j h)", p=NP)
    parts = [(0, MAIN_P), (MAIN_P, NP)]

    with ExitStack() as ctx:
        def sb(name, shape, dt=F32):
            return ctx.enter_context(nc.sbuf_tensor(name, shape, dt))

        def sem(name):
            return ctx.enter_context(nc.semaphore(name))

        xr = sb("xr", [NP, NJ * H])
        hq = sb("hq", [P, NJ * H])
        h_blk = sb("h_blk", [P, 2, BJ * H])
        hT = sb("hT", [P, 2, PAIRS, NP])
        raw_hT = sb("raw_hT", [P, (T + 1) // 2, P])
        sq = sb("sq", [NP, FJ * H])
        mean = sb("mean", [NP, NJ])
        total = sb("total", [NP, NJ])
        var = sb("var", [NP, NJ])
        std = sb("std", [NP, NJ])
        rstd = sb("rstd", [NP, NJ])
        w_edge = sb("w_edge", [KE + 1, T * H])
        w1_pair = sb("w1_pair", [P, 2 * H])
        w3_pair = sb("w3_pair", [P, 2 * H])
        w3a = sb("w3a", [2 * H, H])
        w3b = sb("w3b", [H, H])
        w3bc = sb("w3bc", [H, H])
        w2b = sb("w2b", [H, H + 1])
        w_agg = sb("w_agg", [H + 1, H])
        wsum = sb("wsum", [P, 4])
        b3_row = sb("b3_row", [NP, H])
        b3_c = sb("b3_c", [NP, H])
        scale_row = sb("scale_row", [NP, H])
        bias_row = sb("bias_row", [NP, H])
        eps = sb("eps", [P, 2])
        ident = sb("ident", [P, P])
        iota = sb("iota", [P, W])
        ones = sb("ones", [1, P])
        src_all = sb("src_all", [P, NT + SLOTS * T], I32)
        dst_all = sb("dst_all", [P, NT], I32)
        rel = dst_all[:].bitcast(F32)
        idx = sb("idx", [P, SLOTS, T], I32)
        edge = sb("edge", [KE + 1, MIX, P])
        rows = sb("rows", [P, SLOTS, T * H])
        raw = sb("raw", [P, RAW * T * H])
        raw_total = sb("raw_total", [P, RAW * T])
        raw_mean = sb("raw_mean", [P, RAW * T])
        raw_var = sb("raw_var", [P, RAW * T])
        raw_std = sb("raw_std", [P, RAW * T])
        raw_rstd = sb("raw_rstd", [P, RAW * T])
        msg = sb("msg", [P, 3, T, H + 1])
        hot = sb("hot", [P, T, W])
        seg = sb("seg", [H + 1, W])
        sums_all = sb("sums_all", [P, N + W])
        sums = sums_all[0:H, :]
        t_all = sums_all[0:NP, 0:NJ * H]
        lo_p = sb("lo_p", [P, NCH])
        hi_p = sb("hi_p", [P, NCH])
        lo_q = sb("lo_q", [Q, QS])
        hi_q = sb("hi_q", [Q, QS])
        span_q = sb("span_q", [Q, QS], I32)
        shift_q = sb("shift_q", [Q, QS], I32)
        count_q = sb("count_q", [Q, QS])
        lo_row = sb("lo_row", [1, NCH])
        count_row = sb("count_row", [1, NCH])
        base_tab = sb("base_tab", [1, NCH], I32)
        first_tab = sb("first_tab", [1, NCH + 1], I32)
        big = sb("big", [P, UNITS * UNIT * NP])
        agg_in = big[0:H, :].rearrange("k (u j p) -> k u j p", u=UNITS, j=UNIT)
        raw_sq = big[:, 0:RAW * T * H // 2]
        zero_row = big[0:1, RAW * T * H // 2:RAW * T * H // 2 + NCH]
        raw_h = h_blk[:, 0, 0:T * H]
        RAW_PAIRS = [(q, min(2 * H, (T - 2 * q) * H)) for q in range((T + 1) // 2)]


        psum = ctx.enter_context(nc.psum_tensor("psum", [P, 8 * BANK], F32))

        def bank(b, n=1):
            return psum[:, b * BANK:(b + n) * BANK]

        ps_hT = [bank(2 * s, 2).rearrange("p (i n) -> p i n", n=P) for s in range(2)]
        ps_out = [bank(4 + 2 * s, 2) for s in range(2)]
        ps_base = bank(2, 2)
        ps_lo = bank(4, 2).rearrange("p (i n) -> p i n", n=P)
        ps_hi = bank(6, 2).rearrange("p (i n) -> p i n", n=P)
        ps_edge = [bank(0), bank(5), bank(6)]
        ps_seg = bank(1)
        ps_fold = bank(7)
        ps_q = bank(2, 2)
        ps_rawT = bank(4)
        ps_wagg = bank(1)
        ps_upd = [bank(2 + u) for u in range(UNITS)]

        x_landed = [sem(f"x_landed{s}") for s in range(FB)]
        w_landed, dst_landed, src_landed = sem("w_landed"), sem("dst_landed"), sem("src_landed")
        first_src_landed, raw_landed = sem("first_src_landed"), sem("raw_landed")
        table_stored = sem("table_stored")
        edge_landed = [sem(f"edge_landed{s}") for s in range(MIX)]
        rows_landed = [sem(f"rows_landed{s}") for s in range(SLOTS)]
        ranges_landed, out_stored = sem("ranges_landed"), sem("out_stored")
        filled, consts, w_step, w_scaled = sem("filled"), sem("consts"), sem("w_step"), sem("w_scaled")
        summed, averaged, centred, squared, var_ready, std_ready, rstd_ready = (
            sem("summed"), sem("averaged"), sem("centred"), sem("squared"), sem("var_ready"), sem("std_ready"),
            sem("rstd_ready"))
        h_ready, r_ready = sem("h_ready"), sem("r_ready")
        turned, turned_copied, node_out, t_copied = (
            sem("turned"), sem("turned_copied"), sem("node_out"), sem("t_copied"))
        hT_saved = sem("hT_saved")
        hT_back, q_out, q_ready = sem("hT_back"), sem("q_out"), sem("q_ready")
        wagg_ready, wagg_copied = sem("wagg_ready"), sem("wagg_copied")
        ends_ready, ends_turned, range_step, base_spread, tables_ready = (
            sem("ends_ready"), sem("ends_turned"), sem("range_step"), sem("base_spread"), sem("tables_ready"))
        idx_ready, u_ready, z_ready, msg_ready = sem("idx_ready"), sem("u_ready"), sem("z_ready"), sem("msg_ready")
        sums_zero = sem("sums_zero")
        hot_ready, rel_moved, seg_ready, seg_copied, folded, sums_added = (
            sem("hot_ready"), sem("rel_moved"), sem("seg_ready"), sem("seg_copied"), sem("folded"), sem("sums_added"))
        raw_summed, raw_averaged, raw_centred, raw_squared, raw_var_ready, raw_std_ready, raw_rstd_ready = (
            sem("raw_summed"), sem("raw_averaged"), sem("raw_centred"), sem("raw_squared"), sem("raw_var_ready"),
            sem("raw_std_ready"), sem("raw_rstd_ready"))
        raw_h_ready, raw_turned, raw_copied, raw_z_ready = (
            sem("raw_h_ready"), sem("raw_turned"), sem("raw_copied"), sem("raw_z_ready"))
        agg_copied, upd_ready, y_ready, y_squared, var2_ready, std2_ready, rstd2_ready = (
            sem("agg_copied"), sem("upd_ready"), sem("y_ready"), sem("y_squared"), sem("var2_ready"),
            sem("std2_ready"), sem("rstd2_ready"))
        normed, shifted, gelu_ready, result_ready = sem("normed"), sem("shifted"), sem("gelu_ready"), sem("result_ready")
        last_shifted, last_result_ready = sem("last_shifted"), sem("last_result_ready")

        weights = [(w3a[0:H, :], w3[0:H, :]), (w3a[H:2 * H, :], w3[0:H, :]), (w3b[:], w3[H:2 * H, :]),
                   (w2b[:, 0:H], w2_t), (w2b[:, H:H + 1], b2.rearrange("(k a) -> k a", a=1)),
                   (w1_pair[0:H, 0:H], w1[0:H, :]), (w1_pair[H:2 * H, H:2 * H], w1[0:H, :]),
                   (w_edge[KE:KE + 1, :].rearrange("a (t h) -> a t h", t=T),
                    b1.rearrange("(a t h) -> a t h", a=1, t=1).broadcast_to([1, T, H]))]
        for t in range(T):
            weights.append((w_edge[t * D:(t + 1) * D, t * H:(t + 1) * H], w1[H:H + D, :]))
        for tile, vec in ((b3_row, b3), (scale_row, ln_scale), (bias_row, ln_bias)):
            weights.append((tile[:], vec.rearrange("(a h) -> a h", a=1).broadcast_to([NP, H])))
        W_LANDED = 16 * len(weights)

        def block_cols(b):
            return bass.ds(b * (BJ * H), BJ * H)

        def saved_cols(b):
            return bass.ds(b * (PAIRS * NP), PAIRS * NP)

        def unit_cols(g):
            return bass.ds(g * (UNIT * H), UNIT * H)

        def final_cols(i):
            return bass.ds(i * (FJ * H), FJ * H)

        def over_h(vec, n, parts_n=NP):
            return vec.rearrange("p (j a) -> p j a", a=1).broadcast_to([parts_n, n, H])

        def over_j(row, n):
            return row.rearrange("p (a h) -> p a h", a=1).broadcast_to([NP, n, H])

        def by_node(cols):
            return cols.rearrange("p (j h) -> p j h", h=H)

        squares_at = (sq[:], h_blk[0:NP].rearrange("p s n -> p (s n)"))

        def chunk_of(i, k, mixed):
            return i * MIX + k if mixed else i * SLOTS + RAW + k

        def place(k):
            return 2 if k == SLOTS - 1 else k % 2

        FIRST_SRC = RAW * MIX * T

        block = ctx.enter_context(nc.Block())

        @block.sync
        def _(sp):
            def load_edges(chunk, k):
                sp.dma_start(edge[0:KE, k, :], edge_t[chunk]).then_inc(edge_landed[k], 16)

            sp.dma_start(src_all[:, 0:FIRST_SRC], src_t[:, 0:FIRST_SRC]).then_inc(first_src_landed, 16)
            for g in range(FB):
                for lo, hi in parts:
                    sp.dma_start(xr[lo:hi, final_cols(g)], x_v[lo:hi, final_cols(g)]).then_inc(x_landed[g], 16)
            sp.wait_ge(filled, 3)
            for tile, source in weights:
                sp.dma_start(tile, source).then_inc(w_landed, 16)
            sp.dma_start(src_all[:, FIRST_SRC:NT], src_t[:, FIRST_SRC:NT]).then_inc(src_landed, 16)
            sp.dma_start(dst_all[:], dst_t).then_inc(dst_landed, 16)
            for k in range(MIX):
                load_edges(k, k)

            with sp.Fori(0, NB) as b:
                sp.wait_ge(t_copied, b + 1)
                for lo, hi in parts:
                    sp.dma_start(table_v[lo:hi, block_cols(b)], t_all[lo:hi, block_cols(b)]).then_inc(table_stored, 16)

            sp.wait_ge(range_step, 5)
            sp.dma_start(lo_row[:].rearrange("a (q s) -> a q s", q=Q), lo_q[:]).then_inc(ranges_landed, 16)
            sp.dma_start(count_row[:].rearrange("a (q s) -> a q s", q=Q), count_q[:]).then_inc(ranges_landed, 16)

            def next_edges(i, mixed=False, raw_too=False):
                for k in range(SLOTS + raw_too):
                    c = chunk_of(i, k, mixed)
                    sp.wait_ge(u_ready, c + 1)
                    load_edges(c + (MIX if mixed else SLOTS), k)

            def hT_again(cols):
                sp.dma_start(hT[:, 0, :, :].rearrange("p i n -> p (i n)"), hq[:, cols]).then_inc(hT_back, 16)

            sp.wait_ge(hT_saved, NB)
            sp.wait_ge(node_out, NB)
            hT_again(saved_cols(NB - 1))
            with sp.Fori(0, RAW - 1) as i:
                next_edges(i, mixed=True, raw_too=True)
            next_edges(RAW - 1, mixed=True)
            next_edges(RAW)
            with sp.Fori(RAW + 1, RAW + NB) as i:
                cols = bass.ds(sp.snap(i * -(PAIRS * NP) + (NB - 1 + RAW) * PAIRS * NP), PAIRS * NP)
                sp.wait_ge(q_ready, i - RAW)
                hT_again(cols)
                next_edges(i)
            with sp.Fori(RAW + NB, ROUNDS - 1) as i:
                next_edges(i)

            for i in range(FB):
                if i < FB - 1:
                    sp.wait_ge(result_ready, i + 1)
                else:
                    sp.wait_ge(last_result_ready, 1)
                for lo, hi in parts:
                    sp.dma_start(out_v[lo:hi, final_cols(i)], xr[lo:hi, final_cols(i)]).then_inc(out_stored, 16)
            sp.wait_ge(out_stored, 16 * 2 * FB)

        @block.gpsimd
        def _(pool):
            nc.gpsimd.memset(edge[:], 1.0).then_inc(filled, 1)
            nc.gpsimd.memset(w_edge[:], 0.0).then_inc(filled, 1)
            nc.gpsimd.memset(w1_pair[:], 0.0).then_inc(filled, 1)
            nc.gpsimd.memset(eps[:, 0:1], LN1_EPS).then_inc(filled, 1)
            nc.gpsimd.memset(eps[:, 1:2], LN2_EPS).then_inc(filled, 1)
            nc.gpsimd.memset(src_all[:, NT:NT + SLOTS * T], 0).then_inc(filled, 1)
            nc.gpsimd.memset(w3_pair[:], 0.0).then_inc(filled, 1)
            nc.gpsimd.memset(ident[:], 0.0).then_inc(consts, 1)
            pool.wait_ge(consts, 1)
            nc.gpsimd.affine_select(out=ident[:], in_=ident[:], compare_op=ALU.not_equal, fill=1.0, base=0,
                                    pattern=[[-1, P]], channel_multiplier=1).then_inc(consts, 1)
            nc.gpsimd.iota(iota[:], pattern=[[1, W]], base=0, channel_multiplier=0,
                           allow_small_or_imprecise_dtypes=True).then_inc(consts, 1)
            nc.gpsimd.memset(ones[:], 1.0).then_inc(consts, 1)
            nc.gpsimd.memset(zero_row, 0.0).then_inc(consts, 1)
            nc.gpsimd.memset(first_tab[:, 0:1], 0).then_inc(consts, 1)
            nc.gpsimd.memset(msg[:, :, :, H:H + 1], 1.0).then_inc(consts, 1)

            pool.wait_ge(first_src_landed, 16)
            for r in range(RAW):
                for t in range(T):
                    tile = (r * MIX + SLOTS) * T + t
                    nc.gpsimd.indirect_dma_start(
                        out=raw[:, (r * T + t) * H:(r * T + t + 1) * H], out_offset=None, in_=x,
                        in_offset=bass.IndirectOffsetOnAxis(ap=src_all[:, tile:tile + 1], axis=0),
                    ).then_inc(raw_landed, 16)

            pool.wait_ge(table_stored, 16 * 2 * NB)
            with pool.Fori(0, ROUNDS) as i:
                for k in range(SLOTS):
                    pool.wait_ge(idx_ready, i * SLOTS + k + 1)
                    pool.nop(nofuse=True)
                    for t in range(T):
                        nc.gpsimd.indirect_dma_start(
                            out=rows[:, k, t * H:(t + 1) * H], out_offset=None, in_=table,
                            in_offset=bass.IndirectOffsetOnAxis(ap=idx[:, k, t:t + 1], axis=0),
                        ).then_inc(rows_landed[k], 16)

            pool.wait_ge(r_ready, NB)
            pool.wait_ge(w_landed, W_LANDED)

            def shift(i):
                y = by_node(hq[0:NP, final_cols(i)])
                pool.wait_ge(normed, 2 * i + 2)
                nc.gpsimd.tensor_tensor(y, y, over_j(bias_row[:], FJ), ALU.add).then_inc(shifted, 1)

            def residual(i):
                pool.wait_ge(gelu_ready, i + 1)
                nc.gpsimd.tensor_tensor(xr[:, final_cols(i)], hq[0:NP, final_cols(i)], xr[:, final_cols(i)],
                                        ALU.add).then_inc(result_ready, 1)

            for i in range(FB - 2):
                shift(i)
            for i in range(FB - 1):
                residual(i)

        @block.scalar
        def _(act):
            for g in range(FB):
                act.wait_ge(centred, g + 1)
                if g >= 2:
                    act.wait_ge(var_ready, g - 1)
                nc.scalar.activation(squares_at[g % 2], hq[0:NP, final_cols(g)], ACT.Square).then_inc(squared, 1)
            act.wait_ge(var_ready, FB)
            act.wait_ge(filled, 5)
            nc.scalar.activation(std[:], var[:], ACT.Sqrt, bias=eps[0:NP, 0:1], scale=1.0 / H).then_inc(std_ready, 1)

            def copy_turned(i, s, first):
                act.wait_ge(turned, 2 * i + s + 1)
                if not first:
                    act.wait_ge(node_out, 2 * i + s - 1)
                    act.wait_ge(hT_saved, 2 * i + s - 1)
                nc.scalar.copy(hT[:, s, :, :], ps_hT[s][:, 0:PAIRS, 0:NP]).then_inc(turned_copied, 1)

            def save_turned(i, s):
                act.wait_ge(turned_copied, 2 * i + s + 1)
                nc.scalar.copy(hq[:, saved_cols(2 * i + s)],
                               hT[:, s, :, :].rearrange("p i n -> p (i n)")).then_inc(hT_saved, 1)

            def copy_products(i, s):
                act.wait_ge(node_out, 2 * i + s + 1)
                nc.scalar.copy(t_all[:, block_cols(2 * i + s)], ps_out[s][0:NP, 0:BJ * H]).then_inc(t_copied, 1)

            def node_copies(i, first, last):
                copy_turned(i, 1, first)
                save_turned(i, 0)
                copy_products(i, 0)
                if not last:
                    copy_turned(i + 1, 0, False)
                save_turned(i, 1)
                copy_products(i, 1)

            copy_turned(0, 0, True)
            node_copies(0, True, False)
            with act.Fori(1, NB // 2 - 1) as i:
                node_copies(i, False, False)
            node_copies(NB // 2 - 1, False, True)

            act.wait_ge(src_landed, 16)
            act.wait_ge(filled, 6)
            for k in range(SLOTS):
                nc.scalar.copy(idx[:, k, :], src_all[:, k * T:(k + 1) * T]).then_inc(idx_ready, 1)
            act.wait_ge(table_stored, 16 * 2 * NB)
            nc.scalar.memzero(sums).then_inc(sums_zero, 1)

            for half in range(2):
                act.wait_ge(raw_centred, 1)
                if half:
                    act.wait_ge(raw_var_ready, 1)
                nc.scalar.activation(raw_sq, raw[:, half * (RAW * T * H // 2):(half + 1) * (RAW * T * H // 2)],
                                     ACT.Square).then_inc(raw_squared, 1)
            act.wait_ge(raw_var_ready, 2)
            nc.scalar.activation(raw_std[:], raw_var[:], ACT.Sqrt, bias=eps[:, 0:1],
                                 scale=1.0 / H).then_inc(raw_std_ready, 1)

            act.wait_ge(wagg_ready, 1)
            nc.scalar.copy(w_agg[:], ps_wagg[0:H + 1, 0:H]).then_inc(wagg_copied, 1)

            act.wait_ge(consts, 7)

            def messages(i, mixed):
                for k in range(SLOTS):
                    c = chunk_of(i, k, mixed)
                    act.wait_ge(z_ready, i * SLOTS + k + 1)
                    nc.scalar.activation(msg[:, place(k), :, 0:H], rows[:, k, :].rearrange("p (t h) -> p t h", h=H),
                                         ACT.Gelu_apprx_tanh).then_inc(msg_ready, 1)
                    act.wait_ge(msg_ready, c + 1)
                    next_tile = (c + (MIX if mixed else SLOTS)) * T
                    nc.scalar.copy(idx[:, k, :], src_all[:, bass.ds(next_tile, T)]).then_inc(idx_ready, 1)

            with act.Fori(0, RAW) as i:
                messages(i, True)
                act.wait_ge(raw_turned, i + 1)
                whole = sum(cols == 2 * H for _, cols in RAW_PAIRS) * P
                nc.scalar.copy(raw_hT[:, 0:T // 2, :].rearrange("p q n -> p (q n)"),
                               ps_rawT[:, 0:whole]).then_inc(raw_copied, 1)
                if T % 2:
                    nc.scalar.copy(raw_hT[0:H, T // 2, :], ps_rawT[0:H, whole:whole + P]).then_inc(raw_copied, 1)
                act.wait_ge(raw_z_ready, i + 1)
                nc.scalar.activation(msg[:, place(SLOTS), :, 0:H],
                                     ps_edge[place(SLOTS)][:, 0:T * H].rearrange("p (t h) -> p t h", h=H),
                                     ACT.Gelu_apprx_tanh).then_inc(msg_ready, 1)
            with act.Fori(RAW, ROUNDS) as i:
                messages(i, False)

            windows = act.value_load(first_tab[0:1, NCH:NCH + 1], min_val=NCH, max_val=1 << 20)
            act.wait_ge(sums_added, windows)
            sums_v = sums[:, 0:N].rearrange("k (p j) -> k j p", p=NP)

            def update_copies(i):
                for u in range(UNITS):
                    g = i * UNITS + u
                    if i:
                        act.wait_ge(upd_ready, g - UNITS + 1)
                    nc.scalar.copy(agg_in[:, u, :, :], sums_v[:, g * UNIT:(g + 1) * UNIT, :]).then_inc(agg_copied, 1)

            def gelu(i):
                if i < FB - 2:
                    act.wait_ge(shifted, i + 1)
                else:
                    act.wait_ge(last_shifted, i - (FB - 3))
                nc.scalar.activation(hq[0:NP, final_cols(i)], hq[0:NP, final_cols(i)],
                                     ACT.Gelu_apprx_tanh).then_inc(gelu_ready, 1)

            update_copies(0)
            for i in range(FB):
                act.wait_ge(y_ready, (i + 1) * UNITS)
                if i:
                    act.wait_ge(var2_ready, i)
                nc.scalar.activation(sq[:], hq[0:NP, final_cols(i)], ACT.Square).then_inc(y_squared, 1)
                if i + 1 < FB:
                    update_copies(i + 1)
                act.wait_ge(var2_ready, i + 1)
                js = slice(i * FJ, (i + 1) * FJ)
                nc.scalar.activation(std[:, js], var[:, js], ACT.Sqrt, bias=eps[0:NP, 1:2],
                                     scale=1.0 / H).then_inc(std2_ready, 1)
                if i == FB - 2:
                    for b in range(FB - 3):
                        gelu(b)
            for b in range(max(FB - 3, 0), FB):
                gelu(b)

        @block.tensor
        def _(pe):
            pe.wait_ge(consts, 2)
            pe.wait_ge(w_landed, W_LANDED)

            def turn(b, s):
                pe.wait_ge(h_ready, b + 1)
                for q in range(PAIRS):
                    last = nc.tensor.transpose(ps_hT[s][:, q, 0:NP], h_blk[0:NP, s, q * 2 * H:(q + 1) * 2 * H],
                                               ident[0:NP, 0:NP])
                last.then_inc(turned, 1)

            def products(b, s, first):
                pe.wait_ge(turned_copied, b + 1)
                if not first:
                    pe.wait_ge(t_copied, b - 1)
                for q in range(PAIRS):
                    last = nc.tensor.matmul(ps_out[s][0:NP, q * 2 * H:(q + 1) * 2 * H], hT[:, s, q, :], w1_pair[:],
                                            start=True, stop=True)
                last.then_inc(node_out, 1)

            def node_pair(i, first, last):
                turn(2 * i + 1, 1)
                products(2 * i, 0, first)
                if not last:
                    turn(2 * i + 2, 0)
                products(2 * i + 1, 1, first)

            turn(0, 0)
            node_pair(0, True, False)
            with pe.Fori(1, NB // 2 - 1) as i:
                node_pair(i, False, False)
            node_pair(NB // 2 - 1, False, True)

            pe.wait_ge(t_copied, NB)
            pe.wait_ge(ends_ready, 2)
            for ends, ps in ((lo_p, ps_lo), (hi_p, ps_hi)):
                by_slot = ends[:].rearrange("p (q s) -> p s q", s=QS)
                for s in range(QS):
                    last = nc.tensor.transpose(ps[0:Q, s, :], by_slot[:, s, :], ident[:])
            last.then_inc(ends_turned, 1)
            pe.wait_ge(w_step, 6)
            nc.tensor.matmul(ps_wagg[0:H + 1, 0:H], w2b[:], w3bc[:], start=True, stop=True).then_inc(wagg_ready, 1)
            pe.wait_ge(ranges_landed, 32)
            pe.wait_ge(consts, 4)
            for n in range(0, NCH, BANK):
                m = min(BANK, NCH - n)
                last = nc.tensor.matmul(ps_base[:, n:n + m], ones[:], lo_row[:, n:n + m], start=True, stop=True)
            last.then_inc(base_spread, 1)

            pe.wait_ge(tables_ready, 2)
            pe.wait_ge(wagg_copied, 1)

            def edge_part(i, k):
                pe.wait_ge(edge_landed[k], 16 * i + 16)
                nc.tensor.matmul(ps_edge[place(k)][:, 0:T * H], edge[:, k, :], w_edge[:], start=True,
                                 stop=True).then_inc(u_ready, 1)

            def raw_part(i):
                pe.wait_ge(raw_h_ready, i + 1)
                for q, cols in RAW_PAIRS:
                    last = nc.tensor.transpose(ps_rawT[0:cols, q * P:(q + 1) * P], raw_h[:, q * 2 * H:q * 2 * H + cols],
                                               ident[:])
                last.then_inc(raw_turned, 1)
                z = ps_edge[place(SLOTS)]
                pe.wait_ge(edge_landed[SLOTS], 16 * i + 16)
                nc.tensor.matmul(z[:, 0:T * H], edge[:, SLOTS, :], w_edge[:], start=True, stop=False,
                                 skip_group_check=True).then_inc(u_ready, 1)
                pe.wait_ge(raw_copied, (i + 1) * (1 + T % 2))
                for q, cols in RAW_PAIRS:
                    last = nc.tensor.matmul(z[:, q * 2 * H:q * 2 * H + cols], raw_hT[0:cols, q, :],
                                            w1_pair[0:cols, 0:cols], start=False, stop=(q == len(RAW_PAIRS) - 1),
                                            skip_group_check=True)
                last.then_inc(raw_z_ready, 1)

            def edge_round(i, mixed=False, with_q=False, final=False):
                end = None
                for k in range(MIX if mixed else SLOTS):
                    c = chunk_of(i, k, mixed)
                    if k < SLOTS - 1:
                        edge_part(i, k + 1)
                    elif mixed and k == SLOTS - 1:
                        raw_part(i)
                    elif not final:
                        edge_part(i + 1, 0)
                    first = end
                    if first is None:
                        first = pe.value_load(first_tab[0:1, bass.ds(c, 1)], min_val=0, max_val=1 << 20)
                    end = pe.value_load(first_tab[0:1, bass.ds(c + 1, 1)], min_val=1, max_val=1 << 20)
                    with pe.Fori(first, end) as w:
                        pe.wait_ge(msg_ready, c + 1)
                        pe.wait_ge(hot_ready, w + 1)
                        for t in range(T):
                            last = nc.tensor.matmul(ps_seg[0:H + 1, 0:W], msg[:, place(k), t, :], hot[:, t, :],
                                                    start=(t == 0), stop=(t == T - 1))
                        last.then_inc(seg_ready, 1)
                        pe.wait_ge(seg_copied, w + 1)
                        nc.tensor.matmul(ps_fold[0:H, 0:W], w_agg[:], seg[:], start=True, stop=True).then_inc(folded, 1)
                    if with_q and k == 1:
                        pe.wait_ge(hT_back, 16 * i + (16 - 16 * RAW))
                        for q in range(PAIRS):
                            last = nc.tensor.matmul(ps_q[0:NP, q * 2 * H:(q + 1) * 2 * H], hT[:, 0, q, :], w3_pair[:],
                                                    start=True, stop=True)
                        last.then_inc(q_out, 1)

            edge_part(0, 0)
            with pe.Fori(0, RAW) as i:
                edge_round(i, mixed=True)
            with pe.Fori(RAW, RAW + NB) as i:
                edge_round(i, with_q=True)
            with pe.Fori(RAW + NB, ROUNDS - 1) as i:
                edge_round(i)
            edge_round(ROUNDS - 1, final=True)

            def updates(i, first):
                for u in range(UNITS):
                    g = i * UNITS + u
                    pe.wait_ge(agg_copied, g + 1)
                    if not first:
                        pe.wait_ge(y_ready, g - UNITS + 1)
                    for j in range(UNIT):
                        last = nc.tensor.transpose(ps_upd[u][0:NP, j * H:(j + 1) * H], agg_in[:, u, j, :],
                                                   ident[0:H, 0:H])
                    last.then_inc(upd_ready, 1)

            for i in range(FB):
                updates(i, not i)

        @block.vector
        def _(dve):
            def sum_x_squares(g):
                dve.wait_ge(squared, g + 1)
                nc.vector.tensor_reduce(var[:, g * FJ:(g + 1) * FJ], by_node(squares_at[g % 2]), AX.X,
                                        ALU.add).then_inc(var_ready, 1)

            for g in range(FB):
                js = slice(g * FJ, (g + 1) * FJ)
                dve.wait_ge(x_landed[g], 32)
                nc.vector.tensor_reduce(total[:, js], by_node(xr[:, final_cols(g)]), AX.X, ALU.add).then_inc(summed, 1)
                dve.wait_ge(summed, g + 1)
                nc.vector.tensor_scalar(mean[:, js], total[:, js], 1.0 / H, None, ALU.mult).then_inc(averaged, 1)
                dve.wait_ge(averaged, g + 1)
                nc.vector.tensor_tensor(by_node(hq[0:NP, final_cols(g)]), by_node(xr[:, final_cols(g)]),
                                        over_h(mean[:, js], FJ), ALU.subtract).then_inc(centred, 1)
                if g >= 2:
                    sum_x_squares(g - 2)
            for g in range(FB - 2, FB):
                sum_x_squares(g)

            dve.wait_ge(std_ready, 1)
            nc.vector.reciprocal(rstd[:], std[:]).then_inc(rstd_ready, 1)
            dve.wait_ge(rstd_ready, 1)

            def node_block(i, first):
                for s in range(2):
                    b = 2 * i + s
                    if not first:
                        dve.wait_ge(turned, b - 1)
                        dve.wait_ge(r_ready, b - 1)
                    nc.vector.scalar_tensor_tensor(
                        out=by_node(h_blk[0:NP, s, :]), in0=by_node(hq[0:NP, block_cols(b)]), scalar=0.0,
                        in1=over_h(rstd[:, bass.ds(b * BJ, BJ)], BJ), op0=ALU.max, op1=ALU.mult).then_inc(h_ready, 1)
                for s in range(2):
                    b = 2 * i + s
                    dve.wait_ge(h_ready, b + 1)
                    nc.vector.tensor_tensor(xr[:, block_cols(b)], xr[:, block_cols(b)], h_blk[0:NP, s, :],
                                            ALU.add).then_inc(r_ready, 1)

            node_block(0, True)
            with dve.Fori(1, NB // 2) as i:
                node_block(i, False)

            dve.wait_ge(dst_landed, 16)
            by_chunk = dst_all[:].rearrange("p (c t) -> p c t", t=T)
            nc.vector.tensor_reduce(lo_p[:], by_chunk, AX.X, ALU.min).then_inc(ends_ready, 1)
            nc.vector.tensor_reduce(hi_p[:], by_chunk, AX.X, ALU.max).then_inc(ends_ready, 1)
            dve.wait_ge(w_landed, W_LANDED)
            dve.wait_ge(filled, 7)
            nc.vector.tensor_reduce(wsum[:, 0:1], w3a[:], AX.X, ALU.add).then_inc(w_step, 1)
            nc.vector.tensor_reduce(wsum[0:H, 1:2], w3b[:], AX.X, ALU.add).then_inc(w_step, 1)
            nc.vector.tensor_reduce(wsum[0:NP, 2:3], b3_row[:], AX.X, ALU.add).then_inc(w_step, 1)
            dve.wait_ge(w_step, 3)
            for n, rows_n in enumerate((2 * H, H, NP)):
                sum_n = wsum[0:rows_n, n:n + 1]
                nc.vector.tensor_scalar(sum_n, sum_n, 1.0 / H, None, ALU.mult).then_inc(w_scaled, 1)
            dve.wait_ge(w_scaled, 3)
            nc.vector.tensor_scalar(w3bc[:], w3b[:], wsum[0:H, 1:2], None, ALU.subtract).then_inc(w_step, 1)
            nc.vector.tensor_scalar(b3_c[:], b3_row[:], wsum[0:NP, 2:3], None, ALU.subtract).then_inc(w_step, 1)
            for lo in (0, H):
                last = nc.vector.tensor_scalar(w3_pair[lo:lo + H, lo:lo + H], w3a[lo:lo + H, :],
                                               wsum[lo:lo + H, 0:1], None, ALU.subtract)
            last.then_inc(w_step, 1)

            dve.wait_ge(ends_turned, 1)
            nc.vector.tensor_reduce(lo_q[:], ps_lo[0:Q, 0:QS, :], AX.X, ALU.min).then_inc(range_step, 1)
            nc.vector.tensor_reduce(hi_q[:], ps_hi[0:Q, 0:QS, :], AX.X, ALU.max).then_inc(range_step, 1)
            dve.wait_ge(range_step, 2)
            nc.vector.tensor_tensor(span_q[:], hi_q[:], lo_q[:], ALU.subtract).then_inc(range_step, 1)
            dve.wait_ge(range_step, 3)
            nc.vector.tensor_scalar(shift_q[:], span_q[:], SHIFT, None, ALU.arith_shift_right).then_inc(range_step, 1)
            dve.wait_ge(range_step, 4)
            nc.vector.tensor_scalar(count_q[:], shift_q[:], 1.0, None, ALU.add).then_inc(range_step, 1)
            dve.wait_ge(raw_landed, 16 * T * RAW)
            nc.vector.tensor_reduce(raw_total[:], by_node(raw[:]), AX.X, ALU.add).then_inc(raw_summed, 1)
            dve.wait_ge(raw_summed, 1)
            nc.vector.tensor_scalar(raw_mean[:], raw_total[:], 1.0 / H, None, ALU.mult).then_inc(raw_averaged, 1)
            dve.wait_ge(raw_averaged, 1)
            nc.vector.tensor_tensor(by_node(raw[:]), by_node(raw[:]), over_h(raw_mean[:], RAW * T, P),
                                    ALU.subtract).then_inc(raw_centred, 1)

            def sum_raw_squares(half):
                dve.wait_ge(raw_squared, half + 1)
                nc.vector.tensor_reduce(raw_var[:, half * (RAW * T // 2):(half + 1) * (RAW * T // 2)], by_node(raw_sq),
                                        AX.X, ALU.add).then_inc(raw_var_ready, 1)

            dve.wait_ge(ranges_landed, 32)
            dve.wait_ge(consts, 6)
            nc.vector.tensor_copy(base_tab[:], lo_row[:])
            nc.vector.tensor_tensor_scan(first_tab[:, 1:NCH + 1], count_row[:], zero_row, 0.0,
                                         ALU.add, ALU.add).then_inc(tables_ready, 1)
            sum_raw_squares(0)
            dve.wait_ge(base_spread, 1)
            nc.vector.tensor_tensor(
                rel.rearrange("p (c t) -> p c t", t=T), by_chunk,
                ps_base[:, 0:NCH].rearrange("p (c a) -> p c a", a=1).broadcast_to([P, NCH, T]),
                ALU.subtract).then_inc(tables_ready, 1)
            sum_raw_squares(1)
            dve.wait_ge(raw_std_ready, 1)
            nc.vector.reciprocal(raw_rstd[:], raw_std[:]).then_inc(raw_rstd_ready, 1)
            dve.wait_ge(raw_rstd_ready, 1)
            dve.wait_ge(tables_ready, 2)
            dve.wait_ge(sums_zero, 1)
            dve.wait_ge(consts, 3)

            iota_t = iota[:].rearrange("p (a w) -> p a w", a=1).broadcast_to([P, T, W])

            def argument(i, k, c):
                dve.wait_ge(rows_landed[k], 16 * T * i + 16 * T)
                dve.wait_ge(u_ready, c + 1)
                nc.vector.tensor_tensor(rows[:, k, :], rows[:, k, :], ps_edge[place(k)][:, 0:T * H],
                                        ALU.add).then_inc(z_ready, 1)

            def one_hot(rel_c):
                nc.vector.tensor_tensor(
                    hot[:], rel_c.rearrange("p (t a) -> p t a", a=1).broadcast_to([P, T, W]), iota_t,
                    ALU.is_equal).then_inc(hot_ready, 1)

            def move(rel_c, w):
                dve.wait_ge(hot_ready, w + 1)
                nc.vector.tensor_scalar(rel_c, rel_c, -float(W), None, ALU.add).then_inc(rel_moved, 1)

            def add_window(base, n, w):
                start = nc.s_assert_within(
                    base + n * W, 0, N - 1,
                    skip_runtime_bounds_check_because="the last window starts at or below the highest dst")
                window = sums[:, bass.ds(start, W)]
                dve.wait_ge(seg_ready, w + 1)
                nc.vector.tensor_copy(seg[:], ps_seg[0:H + 1, 0:W]).then_inc(seg_copied, 1)
                dve.wait_ge(folded, w + 1)
                nc.vector.tensor_tensor(window, window, ps_fold[0:H, 0:W], ALU.add).then_inc(sums_added, 1)

            def load_base(c):
                return dve.value_load(base_tab[0:1, bass.ds(c, 1)], min_val=0, max_val=N - 1)

            def load_end(c):
                return dve.value_load(first_tab[0:1, bass.ds(c + 1, 1)], min_val=1, max_val=1 << 20)

            def edge_round(i, mixed=False, with_q=False, final=False):
                steps = MIX if mixed else SLOTS
                c = chunk_of(i, 0, mixed)
                first = dve.value_load(first_tab[0:1, bass.ds(c, 1)], min_val=0, max_val=1 << 20)
                base, end = load_base(c), load_end(c)
                for k in range(steps):
                    c = chunk_of(i, k, mixed)
                    rel_c = rel[:, bass.ds(c * T, T)]
                    one_hot(rel_c)
                    if k < SLOTS - 1:
                        argument(i, k + 1, c + 1)
                    elif not final and k == steps - 1:
                        argument(i + 1, 0, c + 1)
                    if k < steps - 1:
                        next_base, next_end = load_base(c + 1), load_end(c + 1)
                    move(rel_c, first)
                    add_window(base, 0, first)
                    with dve.If(end > first + 1):
                        with dve.Fori(first + 1, end) as w:
                            dve.wait_ge(rel_moved, w)
                            one_hot(rel_c)
                            move(rel_c, w)
                            add_window(base, w - first, w)
                    if k < steps - 1:
                        first, base, end = end, next_base, next_end
                    if mixed and k == 2:
                        nc.vector.scalar_tensor_tensor(
                            out=by_node(raw_h), in0=by_node(raw[:, bass.ds(i * (T * H), T * H)]), scalar=0.0,
                            in1=over_h(raw_rstd[:, bass.ds(i * T, T)], T, P), op0=ALU.max,
                            op1=ALU.mult).then_inc(raw_h_ready, 1)
                    if with_q and k == 2:
                        cols = bass.ds(dve.snap(i * -(BJ * H) + (NB - 1 + RAW) * BJ * H), BJ * H)
                        dve.wait_ge(q_out, i + (1 - RAW))
                        nc.vector.tensor_tensor(by_node(hq[0:NP, cols]), by_node(ps_q[0:NP, 0:BJ * H]),
                                                over_j(b3_c[:], BJ), ALU.add).then_inc(q_ready, 1)

            argument(0, 0, 0)
            with dve.Fori(0, RAW) as i:
                edge_round(i, mixed=True)
            with dve.Fori(RAW, RAW + NB) as i:
                edge_round(i, with_q=True)
            with dve.Fori(RAW + NB, ROUNDS - 1) as i:
                edge_round(i)
            edge_round(ROUNDS - 1, final=True)

            dve.wait_ge(q_ready, NB)

            def add_updates(i):
                for u in range(UNITS):
                    g = i * UNITS + u
                    dve.wait_ge(upd_ready, g + 1)
                    nc.vector.tensor_tensor(hq[0:NP, unit_cols(g)], hq[0:NP, unit_cols(g)], ps_upd[u][0:NP, 0:UNIT * H],
                                            ALU.add).then_inc(y_ready, 1)

            def normalise(i):
                y, js = by_node(hq[0:NP, final_cols(i)]), slice(i * FJ, (i + 1) * FJ)
                dve.wait_ge(std2_ready, i + 1)
                nc.vector.reciprocal(rstd[:, js], std[:, js]).then_inc(rstd2_ready, 1)
                dve.wait_ge(rstd2_ready, i + 1)
                nc.vector.tensor_tensor(y, y, over_h(rstd[:, js], FJ), ALU.mult).then_inc(normed, 1)
                dve.wait_ge(normed, 2 * i + 1)
                nc.vector.tensor_tensor(y, y, over_j(scale_row[:], FJ), ALU.mult).then_inc(normed, 1)

            def shift(i):
                y = by_node(hq[0:NP, final_cols(i)])
                dve.wait_ge(normed, 2 * i + 2)
                nc.vector.tensor_tensor(y, y, over_j(bias_row[:], FJ), ALU.add).then_inc(last_shifted, 1)

            for i in range(FB):
                add_updates(i)
                if i:
                    normalise(i - 1)
                dve.wait_ge(y_squared, i + 1)
                nc.vector.tensor_reduce(var[:, i * FJ:(i + 1) * FJ], by_node(sq[:]), AX.X,
                                        ALU.add).then_inc(var2_ready, 1)
            shift(FB - 2)
            normalise(FB - 1)
            shift(FB - 1)
            dve.wait_ge(gelu_ready, FB)
            nc.vector.tensor_tensor(xr[:, final_cols(FB - 1)], hq[0:NP, final_cols(FB - 1)], xr[:, final_cols(FB - 1)],
                                    ALU.add).then_inc(last_result_ready, 1)


_INS = ["x", "src_t", "dst_t", "edge_t", "w1", "b1", "w2_t", "b2", "w3", "b3", "ln_scale", "ln_bias"]


def kernel(x, src, dst, edge_attr_16, L0_gnn_W1, L0_gnn_b1, L0_gnn_W2, L0_gnn_b2, L0_gnn_W3, L0_gnn_b3,
           L0_gnn_ln_scale, L0_gnn_ln_bias):
    import numpy as np
    import concourse.bacc as bacc
    from concourse.bass_utils import run_bass_kernel_spmd

    x, src, dst, edge_attr = (np.asarray(a) for a in (x, src, dst, edge_attr_16))
    E, D = edge_attr.shape
    chunks = E // (T * P)
    laid = {
        "x": x,
        "src_t": src.reshape(E // P, P).T,
        "dst_t": dst.reshape(E // P, P).T,
        "edge_t": edge_attr.reshape(chunks, T, P, D).transpose(0, 1, 3, 2).reshape(chunks, T * D, P),
        "w1": L0_gnn_W1, "b1": L0_gnn_b1, "w2_t": np.asarray(L0_gnn_W2).T, "b2": L0_gnn_b2,
        "w3": L0_gnn_W3, "b3": L0_gnn_b3, "ln_scale": L0_gnn_ln_scale, "ln_bias": L0_gnn_ln_bias,
    }
    nc = bacc.Bacc("TRN2", target_bir_lowering=False, num_devices=1)
    arrays, args = {}, []
    for name in _INS:
        a = np.ascontiguousarray(laid[name])
        arrays[f"in_{name}"] = a
        args.append(nc.dram_tensor(f"in_{name}", a.shape, mybir.dt.from_np(a.dtype), kind="ExternalInput").ap())
    out = nc.dram_tensor("out", x.shape, F32, kind="ExternalOutput").ap()
    gnn_layer(nc, *args, out)
    result = run_bass_kernel_spmd(nc, [arrays], core_ids=[0])
    return result.results[0]["out"]
```
